# Optimizing a Trainium2 kernel written in Bass

```python
import numpy as np
import jax
import jax.numpy as jnp

def _softmax(x, axis=-1):
    return jax.nn.softmax(x, axis=axis)

def _gelu(x):
    return jax.nn.gelu(x, approximate=True)

def _silu(x):
    return jax.nn.silu(x)

def _sigmoid(x):
    return jax.nn.sigmoid(x)

def _layernorm(x, axis=-1, eps=1e-05):
    m = jnp.mean(x, axis=axis, keepdims=True)
    v = jnp.var(x, axis=axis, keepdims=True)
    return (x - m) / jnp.sqrt(v + eps)

def _scatter_add(tgt, idx, src, axis=0):
    return tgt.at[idx].add(src)

def _segment_sum(src, seg, n):
    return jax.ops.segment_sum(src, seg, n)
kernel_name = 'mk_seq_preln_d1_jaxref_r4_762ed8'

def setup_inputs(seed: int=0):
    np.random.seed(seed)
    _w = jnp.asarray

    def _L0_attn_setup():
        import jax, jax.numpy as jnp
        import numpy as np
        D_MODEL = 256
        D_STATE = 64
        D_CONV = 4
        EXPAND = 2
        HEADDIM = 64
        NGROUPS = 1
        D_INNER = EXPAND * D_MODEL
        NHEADS = D_INNER // HEADDIM
        CONV_CH = D_INNER + 2 * NGROUPS * D_STATE
        D_PROJ = 2 * D_INNER + 2 * NGROUPS * D_STATE + NHEADS
        B_SZ, L_SEQ = (2, 256)

        def _silu(v):
            return v * jax.nn.sigmoid(v)

        def _mamba2(x, Win, convw, convb, dtb, Alog, Dsk, normw, Wout):
            b, l, _ = x.shape
            zxbcdt = x @ Win
            z, xBC, dt = jnp.split(zxbcdt, [D_INNER, D_INNER + CONV_CH], axis=-1)
            xBC = jax.lax.conv_general_dilated(xBC, convw, window_strides=(1,), padding=[(D_CONV - 1, 0)], dimension_numbers=('NLC', 'LIO', 'NLC'), feature_group_count=CONV_CH) + convb
            xBC = _silu(xBC)
            xs, Bm, Cm = jnp.split(xBC, [D_INNER, D_INNER + NGROUPS * D_STATE], axis=-1)
            xs = xs.reshape(b, l, NHEADS, HEADDIM)
            dt = jax.nn.softplus(dt + dtb)
            A = -jnp.exp(Alog)
            dA = jnp.exp(dt * A)

            def step(h, inp):
                dA_t, dt_t, B_t, C_t, x_t = inp
                dBx = jnp.einsum('bh,bn,bhp->bhpn', dt_t, B_t, x_t)
                h = dA_t[:, :, None, None] * h + dBx
                y = jnp.einsum('bn,bhpn->bhp', C_t, h)
                return (h, y)
            h0 = jnp.zeros((b, NHEADS, HEADDIM, D_STATE), x.dtype)
            inps = (jnp.transpose(dA, (1, 0, 2)), jnp.transpose(dt, (1, 0, 2)), jnp.transpose(Bm, (1, 0, 2)), jnp.transpose(Cm, (1, 0, 2)), jnp.transpose(xs, (1, 0, 2, 3)))
            _, ys = jax.lax.scan(step, h0, inps)
            y = jnp.transpose(ys, (1, 0, 2, 3)) + Dsk[None, None, :, None] * xs
            y = y.reshape(b, l, D_INNER)
            y = y * _silu(z)
            y = y * jax.lax.rsqrt(jnp.mean(y * y, axis=-1, keepdims=True) + 1e-05) * normw
            return y @ Wout
        key = jax.random.key(seed)
        ks = jax.random.split(key, 24)
        s = 0.02

        def direction(k0):
            kk = jax.random.split(k0, 8)
            return dict(Win=jax.random.normal(kk[0], (D_MODEL, D_PROJ), jnp.float32) * s, convw=jax.random.normal(kk[1], (D_CONV, 1, CONV_CH), jnp.float32) * 0.1, convb=jnp.zeros((CONV_CH,), jnp.float32), dtb=jnp.log(jnp.expm1(jax.random.uniform(kk[2], (NHEADS,), jnp.float32, 0.001, 0.1))), Alog=jnp.log(jax.random.uniform(kk[3], (NHEADS,), jnp.float32, 1.0, 16.0)), Dsk=jnp.ones((NHEADS,), jnp.float32), normw=jnp.ones((D_INNER,), jnp.float32), Wout=jax.random.normal(kk[4], (D_INNER, D_MODEL), jnp.float32) * s)
        f = direction(ks[0])
        bw = direction(ks[1])
        return {'x': jax.random.normal(ks[2], (B_SZ, L_SEQ, D_MODEL), jnp.float32), 'fWin': f['Win'], 'fconvw': f['convw'], 'fconvb': f['convb'], 'fdtb': f['dtb'], 'fAlog': f['Alog'], 'fD': f['Dsk'], 'fnormw': f['normw'], 'fWout': f['Wout'], 'bWin': bw['Win'], 'bconvw': bw['convw'], 'bconvb': bw['convb'], 'bdtb': bw['dtb'], 'bAlog': bw['Alog'], 'bD': bw['Dsk'], 'bnormw': bw['normw'], 'bWout': bw['Wout'], 'Wo': jax.random.normal(ks[3], (2 * D_MODEL, D_MODEL), jnp.float32) * s, 'bo': jnp.zeros((D_MODEL,), jnp.float32)}
    _L0_attn_in = _L0_attn_setup()

    def _L0_ffn_setup():
        import jax, jax.numpy as jnp
        import numpy as np
        key = jax.random.key(seed)
        k1, k2, k3, k4, k5 = jax.random.split(key, 5)
        d_in, d_out, r = (256, 256, 32)
        x = jax.random.normal(k1, (8, 2048, d_in), dtype=jnp.float32)
        W = jax.random.normal(k2, (d_out, d_in), dtype=jnp.float32) * (1.0 / np.sqrt(d_in))
        b = jax.random.normal(k3, (d_out,), dtype=jnp.float32) * 0.01
        V_r = jax.random.normal(k4, (d_in, r), dtype=jnp.float32) * (1.0 / np.sqrt(d_in))
        C = jax.random.normal(k5, (d_out, r), dtype=jnp.float32) * (1.0 / np.sqrt(r))
        return {'x': x, 'W': W, 'b': b, 'V_r': V_r, 'C': C}
    _L0_ffn_in = _L0_ffn_setup()
    _d = {'L0_attn_x': _L0_attn_in['x'], 'L0_attn_fWin': _L0_attn_in['fWin'], 'L0_attn_fconvw': _L0_attn_in['fconvw'], 'L0_attn_fconvb': _L0_attn_in['fconvb'], 'L0_attn_fdtb': _L0_attn_in['fdtb'], 'L0_attn_fAlog': _L0_attn_in['fAlog'], 'L0_attn_fD': _L0_attn_in['fD'], 'L0_attn_fnormw': _L0_attn_in['fnormw'], 'L0_attn_fWout': _L0_attn_in['fWout'], 'L0_attn_bWin': _L0_attn_in['bWin'], 'L0_attn_bconvw': _L0_attn_in['bconvw'], 'L0_attn_bconvb': _L0_attn_in['bconvb'], 'L0_attn_bdtb': _L0_attn_in['bdtb'], 'L0_attn_bAlog': _L0_attn_in['bAlog'], 'L0_attn_bD': _L0_attn_in['bD'], 'L0_attn_bnormw': _L0_attn_in['bnormw'], 'L0_attn_bWout': _L0_attn_in['bWout'], 'L0_attn_Wo': _L0_attn_in['Wo'], 'L0_attn_bo': _L0_attn_in['bo'], 'L0_ffn_W': _L0_ffn_in['W'], 'L0_ffn_b': _L0_ffn_in['b'], 'L0_ffn_V_r': _L0_ffn_in['V_r'], 'L0_ffn_C': _L0_ffn_in['C']}
    _x0 = _d['L0_attn_x']
    _d['L0_attn_x'] = jax.random.normal(jax.random.fold_in(jax.random.key(seed), 1), (8, 512, 256), dtype=_x0.dtype)
    del _x0
    return _d

def reference(L0_attn_x, L0_attn_fWin, L0_attn_fconvw, L0_attn_fconvb, L0_attn_fdtb, L0_attn_fAlog, L0_attn_fD, L0_attn_fnormw, L0_attn_fWout, L0_attn_bWin, L0_attn_bconvw, L0_attn_bconvb, L0_attn_bdtb, L0_attn_bAlog, L0_attn_bD, L0_attn_bnormw, L0_attn_bWout, L0_attn_Wo, L0_attn_bo, L0_ffn_W, L0_ffn_b, L0_ffn_V_r, L0_ffn_C):

    def _L0_attn_ref(x, fWin, fconvw, fconvb, fdtb, fAlog, fD, fnormw, fWout, bWin, bconvw, bconvb, bdtb, bAlog, bD, bnormw, bWout, Wo, bo):
        import jax, jax.numpy as jnp
        import numpy as np
        D_MODEL = 256
        D_STATE = 64
        D_CONV = 4
        EXPAND = 2
        HEADDIM = 64
        NGROUPS = 1
        D_INNER = EXPAND * D_MODEL
        NHEADS = D_INNER // HEADDIM
        CONV_CH = D_INNER + 2 * NGROUPS * D_STATE
        D_PROJ = 2 * D_INNER + 2 * NGROUPS * D_STATE + NHEADS
        B_SZ, L_SEQ = (2, 256)

        def _silu(v):
            return v * jax.nn.sigmoid(v)

        def _mamba2(x, Win, convw, convb, dtb, Alog, Dsk, normw, Wout):
            b, l, _ = x.shape
            zxbcdt = x @ Win
            z, xBC, dt = jnp.split(zxbcdt, [D_INNER, D_INNER + CONV_CH], axis=-1)
            xBC = jax.lax.conv_general_dilated(xBC, convw, window_strides=(1,), padding=[(D_CONV - 1, 0)], dimension_numbers=('NLC', 'LIO', 'NLC'), feature_group_count=CONV_CH) + convb
            xBC = _silu(xBC)
            xs, Bm, Cm = jnp.split(xBC, [D_INNER, D_INNER + NGROUPS * D_STATE], axis=-1)
            xs = xs.reshape(b, l, NHEADS, HEADDIM)
            dt = jax.nn.softplus(dt + dtb)
            A = -jnp.exp(Alog)
            dA = jnp.exp(dt * A)

            def step(h, inp):
                dA_t, dt_t, B_t, C_t, x_t = inp
                dBx = jnp.einsum('bh,bn,bhp->bhpn', dt_t, B_t, x_t)
                h = dA_t[:, :, None, None] * h + dBx
                y = jnp.einsum('bn,bhpn->bhp', C_t, h)
                return (h, y)
            h0 = jnp.zeros((b, NHEADS, HEADDIM, D_STATE), x.dtype)
            inps = (jnp.transpose(dA, (1, 0, 2)), jnp.transpose(dt, (1, 0, 2)), jnp.transpose(Bm, (1, 0, 2)), jnp.transpose(Cm, (1, 0, 2)), jnp.transpose(xs, (1, 0, 2, 3)))
            _, ys = jax.lax.scan(step, h0, inps)
            y = jnp.transpose(ys, (1, 0, 2, 3)) + Dsk[None, None, :, None] * xs
            y = y.reshape(b, l, D_INNER)
            y = y * _silu(z)
            y = y * jax.lax.rsqrt(jnp.mean(y * y, axis=-1, keepdims=True) + 1e-05) * normw
            return y @ Wout
        out_fwd = _mamba2(x, fWin, fconvw, fconvb, fdtb, fAlog, fD, fnormw, fWout)
        x_rev = jnp.flip(x, axis=1)
        out_rev = _mamba2(x_rev, bWin, bconvw, bconvb, bdtb, bAlog, bD, bnormw, bWout)
        out_rev = jnp.flip(out_rev, axis=1)
        out = jnp.concatenate([out_fwd, out_rev], axis=-1) @ Wo + bo
        return out

    def _L0_ffn_ref(x, W, b, V_r, C):
        import jax, jax.numpy as jnp
        import numpy as np
        base = jnp.einsum('bsd,od->bso', x, W) + b
        correction = jnp.einsum('bsr,or->bso', jnp.einsum('bsd,dr->bsr', x, V_r), C)
        return base + correction
    x = L0_attn_x
    x = x + _L0_attn_ref(_layernorm(x, axis=-1), L0_attn_fWin, L0_attn_fconvw, L0_attn_fconvb, L0_attn_fdtb, L0_attn_fAlog, L0_attn_fD, L0_attn_fnormw, L0_attn_fWout, L0_attn_bWin, L0_attn_bconvw, L0_attn_bconvb, L0_attn_bdtb, L0_attn_bAlog, L0_attn_bD, L0_attn_bnormw, L0_attn_bWout, L0_attn_Wo, L0_attn_bo)
    x = x + _L0_ffn_ref(_layernorm(x, axis=-1), L0_ffn_W, L0_ffn_b, L0_ffn_V_r, L0_ffn_C)
    return x

_drawn_inputs = setup_inputs


def setup_inputs(seed=0):
    import zlib

    import numpy as np

    out = dict(_drawn_inputs(seed))
    spreads = {'L0_attn_fconvb': (0.0, 0.1),
     'L0_attn_fD': (1.0, 0.2),
     'L0_attn_fnormw': (1.0, 0.2),
     'L0_attn_bconvb': (0.0, 0.1),
     'L0_attn_bD': (1.0, 0.2),
     'L0_attn_bnormw': (1.0, 0.2),
     'L0_attn_bo': (0.0, 0.1)}
    factors = {'L0_attn_fdtb': 8.0,
     'L0_attn_fAlog': 8.0,
     'L0_attn_bdtb': 8.0,
     'L0_attn_bAlog': 8.0,
     'L0_ffn_b': 8.0}
    for name, (base, spread) in spreads.items():
        noise = np.random.default_rng([zlib.crc32(name.encode()), seed]).standard_normal(out[name].shape)
        drawn = base * np.exp(spread * noise) if base else spread * noise
        out[name] = jnp.asarray(drawn.astype(out[name].dtype))
    for name, factor in factors.items():
        out[name] = (out[name] * factor).astype(out[name].dtype)
    return out
```

```python
from contextlib import ExitStack

import concourse.bass as bass
from concourse import mybir

F32 = mybir.dt.float32
F32R = mybir.dt.float32r
BF16 = mybir.dt.bfloat16
ALU = mybir.AluOpType
ACT = mybir.ActivationFunctionType

P = 128
NB, T, D = 8, 512, 256
DI, NS, NH, HP = 512, 64, 8, 64
KW = 4
DPROJ = 2 * DI + 2 * NS + NH
Q = 128
NC = T // Q
KD = D // P
KI = DI // P
RANK = 32
EPS = 1e-5
A_FLOOR = -105.0
FAR = -32768.0
PIECES = 3

COLS = [2 * DI] + [DI + P * t for t in range(KI)] + [P * t for t in range(KI)]
NCONV = 1 + KI
NT = len(COLS)

ORDER = [list(range(NC)), list(reversed(range(NC)))]
BEFORE_LOOP = 2 * KI + KD

BC = ["h0", "h1", "p0", "h2", "h3", "p1", "h4", "h5", "p2", "h6", "h7", "p3"]

SSD = ["bt"] + [f"x{j}" for j in range(NC)] + ["g", "s0", "s1", "s2"]
FIRST = ["a0", "a1", "dtm", "dtt", "S", "ST"]
LOOP = ([f"0{n}" for n in SSD] + ["a0", "a1", "0ss"] + [f"1{n}" for n in SSD] + ["dtm", "dtt", "1ss", "o0", "o1", "o2", "o3"]
        + ["S", "t0", "t1", "f0", "f1", "ST", "t2", "t3", "f2", "f3"])
LAST = ([f"0{n}" for n in SSD] + ["0ss"] + [f"1{n}" for n in SSD] + ["1ss", "o0", "o1", "o2", "o3"]
        + ["t0", "t1", "f0", "f1", "t2", "t3", "f2", "f3"])
LOOP_BASE = BEFORE_LOOP + len(FIRST)
assert LOOP_BASE % 2 == 0 and len(LOOP) % 2 == 0


def misc_use(phase, it, name):
    if phase == "weights":
        n = name
        return n % 2, n // 2
    if phase == "first":
        n = BEFORE_LOOP + FIRST.index(name)
        return n % 2, n // 2
    if phase == "loop":
        n = LOOP_BASE + LOOP.index(name)
        return n % 2, it * (len(LOOP) // 2) + n // 2
    n = LOOP_BASE + (NB - 1) * len(LOOP) + LAST.index(name)
    return n % 2, n // 2


def build(nc, x, consts, selcol, win, convw, convb, dtb, alog, dskip, normw, woutT, wo, bo, ffT, ffb, vrT, cT, out):
    with ExitStack() as ctx:
        def sb(name, shape, dt=F32):
            return ctx.enter_context(nc.sbuf_tensor(name, shape, dt))

        def sem(name):
            return ctx.enter_context(nc.semaphore(name))

        cst = sb("cst", [P, 4, P])
        ident, upto, since, ones = (cst[:, i, :] for i in range(4))
        tri = [upto, since]
        identb = sb("identb", [P, P], BF16)
        selc = sb("selc", [NS, 2 * NH])
        sel = sb("sel", [NS, 2 * NH, P], BF16)
        selp = sb("selp", [NS, 2 * NH, HP], BF16)
        hide = sb("hide", [P, 2, Q], BF16)
        halves = sb("halves", [P, 16])
        w_hi = sb("w_hi", [P, 2, KD, DPROJ - NH], F32R)
        w_lo = sb("w_lo", [P, 2, KD, DPROJ - NH], F32R)
        wdt_hi = sb("wdt_hi", [P, KD, P], F32R)
        wdt_lo = sb("wdt_lo", [P, KD, P], F32R)
        cw = sb("cw", [P, 2, NCONV, KW])
        cb = sb("cb", [P, 2, NCONV])
        dtb_sb = sb("dtb_sb", [2 * NH, 1])
        arow = sb("arow", [P, 2 * NH])
        abc = sb("abc", [P, NC, 2 * NH])
        dsk = sb("dsk", [P, 2, KI])
        nw = sb("nw", [P, 2, KI])
        wc = sb("wc", [P, 2, KI, D])
        wff = sb("wff", [P, KD, D])
        bo_sb = sb("bo_sb", [P, D])
        ffb_sb = sb("ffb_sb", [P, D])

        xin = sb("xin", [P, NC, D])
        xres = sb("xres", [P, NC, D])
        st1 = sb("st1", [P, NC, 6])
        mv1 = sb("mv1", [P, NC, 2])
        ve1 = sb("ve1", [P, NC])
        rstd1 = sb("rstd1", [P, NC])
        xn = sb("xn", [P, NC, D])
        xnt_hi = sb("xnt_hi", [P, KD, T], F32R)
        xnt_lo = sb("xnt_lo", [P, KD, T], F32R)
        NCH = NC * 2 * NH
        v, na, e, u1, lnu, du, dd, rq, r1, r2, r3, dt, adt, al = (
            sb(n, [P, NCH]) for n in "v na e u1 lnu du dd rq r1 r2 r3 dt adt al".split())
        s_all = sb("s_all", [P, 2 * NCH])
        neg_s = sb("neg_s", [P, NCH])
        wd = sb("wd", [P, NCH])
        w_end = sb("w_end", [P, NCH])
        e_end = sb("e_end", [P, NCH])
        rem1 = sb("rem1", [P, NCH])
        rem2 = sb("rem2", [P, NCH])
        spc = sb("spc", [P, NC, NS], BF16)
        st_bf = sb("st_bf", [NS, T], BF16)
        ss = sb("ss", [P, 2, NC])
        ms = sb("ms", [P, 2 * NC])
        rms = sb("rms", [P, 2 * NC])
        st2 = sb("st2", [P, NC, 6])
        mv2 = sb("mv2", [P, NC, 2])
        ve2 = sb("ve2", [P, NC])
        rstd2 = sb("rstd2", [P, NC])
        xn2 = xn
        xn2t = sb("xn2t", [P, 2, KD, P])
        ot = sb("ot", [P, NC, D])

        xc = sb("xc", [P, 3, T])
        xs = sb("xs", [P, 2, KI, T])
        bcm = sb("bcm", [P, 2, T])
        cc = sb("cc", [P, 2, T])
        sz = sb("sz", [P, 2, KI, T])
        xdt = sb("xdt", [P, NC, DI])
        xw = sb("xw", [P, NC - 1, DI])
        btok = sb("btok", [P, NC, 2, NS])
        gm = sb("gm", [P, T])
        dt_t = gm[0:2 * NH, :]
        lx = sb("lx", [P, 2, T])
        mx = sb("mx", [P, 4, T])
        es = sb("es", [P, 2, T])
        c2 = sb("c2", [P, 2, T])
        hst = sb("hst", [P, NC - 1, KI, P])
        hs = sb("hs", [P, KI, P])
        yt = sb("yt", [P, T])
        yg = sb("yg", [P, 2, KI, T])
        sq = sb("sq", [P, T])
        sqsum = sb("sqsum", [P, T])

        raw_w = [yg[:].rearrange("p a b t -> p (a b t)")[:, 0:KD * DPROJ].rearrange("p (k n) -> p k n", k=KD),
                 sz[:].rearrange("p a b t -> p (a b t)")[:, 0:KD * DPROJ].rearrange("p (k n) -> p k n", k=KD)]
        wdt = hs[:, 0:KD, :]
        raw_woutT = xdt[:].rearrange("p c (k n) -> p c k n", k=1)[:, :, 0, :]
        raw_wo = xw[:].rearrange("p c n -> p (c n)")[:, 0:4 * D].rearrange("p (m n) -> p m n", m=4)
        raw_ffT = mx[:].rearrange("p c n -> p (c n)")[:, 0:KD * D].rearrange("p (k n) -> p k n", k=KD)
        raw_vrT = mx[0:RANK, 2, 0:D]
        raw_cT = mx[0:RANK, 2, D:2 * D]

        def banks(name, n):
            return [ctx.enter_context(nc.psum_tensor(f"{name}{i}", [P, T], F32)) for i in range(n)]

        pj, sbk, py, mi = banks("pj", 2), banks("sbk", 2), banks("py", 2), banks("mi", 2)

        def ring(name):
            return [sem(f"{name}_full{i}") for i in range(2)], [sem(f"{name}_free{i}") for i in range(2)]

        pj_full, pj_free = ring("pj")
        sb_full, sb_free = ring("sb")
        py_full, py_free = ring("py")
        mi_full, mi_free = ring("mi")

        (passed, w_loaded, c_loaded, setup_done, sel_done, wsplit_hi, wsplit_lo, a_exp, a_done, x_loaded, ln1_stats,
         ln1_mv, ln1_ve, ln1_rstd, xn_ready, xnt_hi_ready, xres_ready, na_ready, e_ready, u_ready, ln_ready,
         dt_step, al_ready, s_ready, negs_ready, wd_ready, w_ready, spc_step, spc_ready, conv_first,
         conv_step, bc_ready,  xs_ready, xw_ready, m_ready, c2_ready, hs_ready, yg_ready, sq_step,
         sqsum_ready, ms_ready, rms_ready, x1_step, ln2_stats, ln2_mv, ln2_ve, ln2_rstd, xn2_ready,
         otb_ready, out_stored) = (sem(n) for n in (
            "passed w_loaded c_loaded setup_done sel_done wsplit_hi wsplit_lo a_exp a_done x_loaded ln1_stats ln1_mv "
            "ln1_ve ln1_rstd xn_ready xnt_hi_ready xres_ready na_ready e_ready u_ready ln_ready dt_step al_ready "
            "s_ready negs_ready wd_ready w_ready spc_step spc_ready conv_first conv_step bc_ready "
            "xs_ready xw_ready m_ready c2_ready hs_ready yg_ready sq_step sqsum_ready ms_ready rms_ready x1_step "
            "ln2_stats ln2_mv ln2_ve ln2_rstd xn2_ready otb_ready out_stored").split())

        cc_loaded = [sem("cc_loaded_f"), sem("cc_loaded_b")]

        def pj_use(b, d, t):
            n = NT * d + t
            return n % 2, b * NT + n // 2

        def sb_use(b, d, name):
            n = len(BC) * d + BC.index(name)
            return n % 2, b * len(BC) + n // 2

        def py_use(b, d, p):
            n = KI * d + p
            return n % 2, b * KI + n // 2

        def alone(eng):
            eng.sem_inc(passed, 1)

        block = ctx.enter_context(nc.Block())

        @block.sync
        def _(sp):
            for dst, src in ((cst[:], consts), (selc[:], selcol)):
                sp.dma_start(dst, src).then_inc(c_loaded, 16)
            sp.dma_start(xin[:], x[0].rearrange("(c p) d -> p c d", p=P)).then_inc(x_loaded, 16)
            for d in range(2):
                sp.dma_start(raw_w[d], win[d].rearrange("(k p) n -> p k n", p=P)).then_inc(w_loaded, 16)
                sp.dma_start(wdt[:, :, NH * d:NH * d + NH],
                             win[d][:, DPROJ - NH:DPROJ].rearrange("(k p) n -> p k n", p=P)).then_inc(c_loaded, 16)
                sp.dma_start(cw[:, d], convw[d]).then_inc(c_loaded, 16)
                sp.dma_start(cb[:, d], convb[d]).then_inc(c_loaded, 16)
                sp.dma_start(dtb_sb[NH * d:NH * d + NH, :], dtb[d].rearrange("(h o) -> h o", o=1)).then_inc(c_loaded, 16)
                sp.dma_start(arow[:, NH * d:NH * d + NH], alog[d].partition_broadcast(P)).then_inc(c_loaded, 16)
                sp.dma_start(nw[:, d], normw[d]).then_inc(c_loaded, 16)
                for e2 in range(2):
                    sp.dma_start(dsk[HP * e2:HP * e2 + HP, d, :],
                                 dskip[d][e2].partition_broadcast(HP)).then_inc(c_loaded, 16)
                sp.dma_start(raw_woutT[:, 2 * d:2 * d + 2, :],
                             woutT[d].rearrange("(m p) n -> p m n", p=P)).then_inc(w_loaded, 16)
            sp.dma_start(raw_wo, wo.rearrange("(m p) n -> p m n", p=P)).then_inc(w_loaded, 16)
            sp.dma_start(raw_ffT, ffT.rearrange("(k p) n -> p k n", p=P)).then_inc(w_loaded, 16)
            sp.dma_start(raw_vrT, vrT).then_inc(w_loaded, 16)
            sp.dma_start(raw_cT, cT).then_inc(w_loaded, 16)
            sp.dma_start(bo_sb[:], bo.partition_broadcast(P)).then_inc(w_loaded, 16)
            sp.dma_start(ffb_sb[:], ffb.partition_broadcast(P)).then_inc(w_loaded, 16)

            def copy_c(b, d):
                sp.wait_ge(bc_ready, 2 * b + d + 1)
                sp.dma_start(cc[0:NS, d, :], bcm[NS:P, d, :]).then_inc(cc_loaded[d], 16)
                sp.dma_start(cc[NS:P, d, :], bcm[NS:P, d, :]).then_inc(cc_loaded[d], 16)

            def store(phase, it, b):
                for c in range(NC):
                    bank, used = misc_use(phase, it, f"f{c}")
                    sp.wait_ge(mi_free[bank], used + 2)
                    alone(sp)
                    sp.dma_start(out[b, Q * c:Q * c + Q, :], ot[:, c, :]).then_inc(out_stored, 16)

            copy_c(0, 0)
            copy_c(0, 1)
            with sp.Fori(0, NB - 1) as it:
                sp.wait_ge(xn_ready, NC * it + NC)
                alone(sp)
                sp.wait_ge(xres_ready, it + 1)
                alone(sp)
                sp.dma_start(xin[:], x[it + 1].rearrange("(c p) d -> p c d", p=P)).then_inc(x_loaded, 16)
                copy_c(it + 1, 0)
                copy_c(it + 1, 1)
                store("loop", it, it)
            store("last", 0, NB - 1)
            sp.wait_ge(out_stored, 16 * NC * NB + 1)

        @block.tensor
        def _(pe):
            def misc(phase, it, name):
                bank, used = misc_use(phase, it, name)
                pe.wait_ge(mi_free[bank], used + 1)
                return mi[bank], mi_full[bank]

            def fold_weights():
                pe.wait_ge(c_loaded, 16 * (2 + 2 * 8))
                pe.wait_ge(w_loaded, 16 * 10)
                n = 0
                for d in range(2):
                    for t in range(KI):
                        ps, full = misc("weights", 0, n)
                        for m in range(KD):
                            mm = pe.matmul(ps[:, 0:D], raw_woutT[:, 2 * d + m, P * t:P * t + P], raw_wo[:, 2 * d + m, :],
                                           start=(m == 0), stop=(m == KD - 1))
                        mm.then_inc(full, 1)
                        n += 1
                for k in range(KD):
                    ps, full = misc("weights", 0, n)
                    pe.matmul(ps[:, 0:D], raw_vrT[:, P * k:P * k + P], raw_cT, start=True, stop=True).then_inc(full, 1)
                    n += 1

            def norm_transposed(phase, it, b):
                pe.wait_ge(xn_ready, NC * b + NC)
                for k in range(KD):
                    ps, full = misc(phase, it, f"a{k}")
                    for c in range(NC):
                        mm = pe.transpose(ps[:, Q * c:Q * c + Q], xn[:, c, P * k:P * k + P], ident)
                    mm.then_inc(full, 1)

            def released(phase, it, name):
                bank, used = misc_use(phase, it, name)
                pe.wait_ge(mi_free[bank], used + 2)

            def wait_xnt(phase, it):
                for k in range(KD):
                    released(phase, it, f"a{k}")

            def three_passes(ps, hi, lo):
                for k in range(KD):
                    pe.matmul(ps[:], hi(k), xnt_hi[:, k, :], start=(k == 0), stop=False)
                    pe.matmul(ps[:], hi(k), xnt_lo[:, k, :], start=False, stop=False)
                    mm = pe.matmul(ps[:], lo(k), xnt_hi[:, k, :], start=False, stop=(k == KD - 1))
                return mm

            def project(b, d, t):
                bank, used = pj_use(b, d, t)
                pe.wait_ge(pj_free[bank], used + 1)
                c0 = COLS[t]
                three_passes(pj[bank], lambda k: w_hi[:, d, k, c0:c0 + P],
                             lambda k: w_lo[:, d, k, c0:c0 + P]).then_inc(pj_full[bank], 1)

            def dt_project(phase, it):
                ps, full = misc(phase, it, "dtm")
                three_passes(ps, lambda k: wdt_hi[:, k, :], lambda k: wdt_lo[:, k, :]).then_inc(full, 1)

            def dt_transposed(phase, it):
                released(phase, it, "dtm")
                ps, full = misc(phase, it, "dtt")
                alone(pe)
                for c in range(NC):
                    mm = pe.transpose(ps[:, 2 * NH * c:2 * NH * (c + 1)], dt_t[:, Q * c:Q * c + Q], ident[0:2 * NH, 0:2 * NH])
                mm.then_inc(full, 1)

            def sums(phase, it, b):
                pe.wait_ge(al_ready, b + 1)
                ps, full = misc(phase, it, "S")
                av = al[:].rearrange("p (c d h) -> p d c h", d=2, h=NH)
                for d in range(2):
                    pe.matmul(ps[:, NC * NH * d:NC * NH * (d + 1)], tri[d], av[:, d], start=True, stop=True)
                pe.matmul(ps[:, NCH:2 * NCH], ones, al[:], start=True, stop=True).then_inc(full, 1)

            def s_transposed(phase, it, b):
                pe.wait_ge(spc_ready, b + 1)
                ps, full = misc(phase, it, "ST")
                alone(pe)
                pb = ps[0:NS, 0:T // 2].bitcast(BF16)
                for c in range(NC):
                    mm = pe.transpose(pb[:, Q * c:Q * c + Q], spc[:, c, :], identb[:])
                mm.then_inc(full, 1)

            def spread(b, d, name):
                bank, used = sb_use(b, d, name)
                pe.wait_ge(sb_free[bank], used + 1)
                n = int(name[1])
                w = sel[:, NH * d + n, :] if name[0] == "h" else selp[:, NH * d + 2 * n:NH * d + 2 * n + 2, :]
                mm = pe.matmul(sbk[bank][:], w, st_bf[:], start=True, stop=(name[0] == "p"))
                if name[0] == "h":
                    mm = pe.matmul(sbk[bank][:], identb[:], hide[:, d, :].unsqueeze(1).broadcast_to([P, NC, Q]),
                                   start=False, stop=True)
                mm.then_inc(sb_full[bank], 1)

            def b_tokens(phase, it, d):
                ps, full = misc(phase, it, f"{d}bt")
                alone(pe)
                for c in range(NC):
                    mm = pe.transpose(ps[:, NS * c:NS * c + NS], bcm[0:NS, d, Q * c:Q * c + Q], ident[0:NS, 0:NS])
                mm.then_inc(full, 1)

            def x_tokens(phase, it, d, j):
                ps, full = misc(phase, it, f"{d}x{j}")
                c = ORDER[d][j]
                for t in range(KI):
                    mm = pe.transpose(ps[:, P * t:P * t + P], xs[:, d, t, Q * c:Q * c + Q], ident)
                mm.then_inc(full, 1)

            def scores(phase, it, b, d):
                pe.wait_ge(cc_loaded[d], 32 * (b + 1))
                ps, full = misc(phase, it, f"{d}g")
                for c in range(NC):
                    mm = pe.matmul(ps[:, Q * c:Q * c + Q], bcm[0:NS, d, Q * c:Q * c + Q], cc[0:NS, d, Q * c:Q * c + Q],
                                   start=True, stop=True)
                mm.then_inc(full, 1)

            def state(phase, it, b, d, j):
                u = 2 * b + d
                if j == 0:
                    released(phase, it, f"{d}bt")
                pe.wait_ge(xw_ready, (NC - 1) * u + j + 1)
                ps, full = misc(phase, it, f"{d}s{j}")
                pe.matmul(ps[:], btok[:, ORDER[d][j], :, :], xw[:, j, :], start=True, stop=True).then_inc(full, 1)

            def outputs(phase, it, b, d, p):
                u = 2 * b + d
                bank, used = py_use(b, d, p)
                pe.wait_ge(py_free[bank], used + 1)
                pe.wait_ge(m_ready, 2 + NH * u + 2 * p + 2)
                for c in range(NC):
                    for half in range(2):
                        h = 2 * p + half
                        pe.matmul(py[bank][HP * half:HP * half + HP, Q * c:Q * c + Q], xdt[:, c, HP * h:HP * h + HP],
                                  mx[:, h % 4, Q * c:Q * c + Q], start=(c == 0), stop=False, skip_group_check=True)
                if p == 0:
                    released(phase, it, f"{d}s{NC - 2}")
                pe.wait_ge(c2_ready, 2 + KI * u + p + 1)
                for j in range(NC - 1):
                    c = ORDER[d][j + 1]
                    mm = pe.matmul(py[bank][:, Q * c:Q * c + Q], hst[:, j, p, :], c2[:, p % 2, Q * c:Q * c + Q],
                                   start=False, stop=(j == NC - 2), skip_group_check=True)
                mm.then_inc(py_full[bank], 1)

            def squares(phase, it, b, d):
                pe.wait_ge(sqsum_ready, 2 * b + d + 1)
                ps, full = misc(phase, it, f"{d}ss")
                for c in range(NC):
                    mm = pe.matmul(ps[:, c:c + 1], sqsum[:, Q * c:Q * c + Q], ones[:, 0:1], start=True, stop=True)
                mm.then_inc(full, 1)

            def mix(phase, it, b, c):
                if c == 0:
                    pe.wait_ge(yg_ready, 2 * KI * (b + 1))
                ps, full = misc(phase, it, f"o{c}")
                for d in range(2):
                    for t in range(KI):
                        mm = pe.matmul(ps[:, D * d:D * d + D], yg[:, d, t, Q * c:Q * c + Q], wc[:, d, t, :],
                                       start=(t == 0), stop=(t == KI - 1))
                mm.then_inc(full, 1)

            def norm2_transposed(phase, it, b, c):
                pe.wait_ge(xn2_ready, NC * b + c + 1)
                ps, full = misc(phase, it, f"t{c}")
                for k in range(KD):
                    mm = pe.transpose(ps[:, P * k:P * k + P], xn2[:, c, P * k:P * k + P], ident)
                mm.then_inc(full, 1)

            def feed(phase, it, c):
                released(phase, it, f"t{c}")
                ps, full = misc(phase, it, f"f{c}")
                for k in range(KD):
                    mm = pe.matmul(ps[:, 0:D], xn2t[:, c % 2, k, :], wff[:, k, :], start=(k == 0), stop=(k == KD - 1))
                mm.then_inc(full, 1)

            def scan(phase, it, b, d, between):
                spread(b, d, "h0")
                spread(b, d, "h1")
                pe.wait_ge(bc_ready, 2 * b + d + 1)
                b_tokens(phase, it, d)
                pe.wait_ge(xs_ready, KI * (2 * b + d + 1))
                for j in range(NC):
                    x_tokens(phase, it, d, j)
                scores(phase, it, b, d)
                spread(b, d, "p0")
                spread(b, d, "h2")
                state(phase, it, b, d, 0)
                spread(b, d, "h3")
                state(phase, it, b, d, 1)
                spread(b, d, "p1")
                spread(b, d, "h4")
                state(phase, it, b, d, 2)
                outputs(phase, it, b, d, 0)
                spread(b, d, "h5")
                spread(b, d, "p2")
                between()
                outputs(phase, it, b, d, 1)
                spread(b, d, "h6")
                spread(b, d, "h7")
                spread(b, d, "p3")
                outputs(phase, it, b, d, 2)
                outputs(phase, it, b, d, 3)

            fold_weights()
            norm_transposed("first", 0, 0)
            wait_xnt("first", 0)
            pe.wait_ge(wsplit_hi, 3)
            pe.wait_ge(wsplit_lo, 3)
            for t in range(NT):
                project(0, 0, t)
            dt_project("first", 0)
            project(0, 1, 0)
            dt_transposed("first", 0)
            project(0, 1, 1)
            project(0, 1, 2)
            sums("first", 0, 0)
            project(0, 1, 3)
            s_transposed("first", 0, 0)
            for t in range(4, NT):
                project(0, 1, t)
            released("first", 0, "ST")

            with pe.Fori(0, NB - 1) as it:
                nxt = it + 1
                scan("loop", it, it, 0, lambda: norm_transposed("loop", it, nxt))
                wait_xnt("loop", it)
                for t in range(NT):
                    project(nxt, 0, t)
                squares("loop", it, it, 0)
                scan("loop", it, it, 1, lambda: None)
                dt_project("loop", it)
                project(nxt, 1, 0)
                dt_transposed("loop", it)
                project(nxt, 1, 1)
                squares("loop", it, it, 1)
                mix("loop", it, it, 0)
                mix("loop", it, it, 1)
                project(nxt, 1, 2)
                mix("loop", it, it, 2)
                mix("loop", it, it, 3)
                sums("loop", it, nxt)
                project(nxt, 1, 3)
                norm2_transposed("loop", it, it, 0)
                norm2_transposed("loop", it, it, 1)
                project(nxt, 1, 4)
                feed("loop", it, 0)
                feed("loop", it, 1)
                s_transposed("loop", it, nxt)
                project(nxt, 1, 5)
                norm2_transposed("loop", it, it, 2)
                norm2_transposed("loop", it, it, 3)
                project(nxt, 1, 6)
                feed("loop", it, 2)
                feed("loop", it, 3)
                project(nxt, 1, 7)
                project(nxt, 1, 8)
                released("loop", it, "ST")

            b = NB - 1
            scan("last", 0, b, 0, lambda: None)
            squares("last", 0, b, 0)
            scan("last", 0, b, 1, lambda: None)
            squares("last", 0, b, 1)
            for c in range(NC):
                mix("last", 0, b, c)
            for c0 in (0, 2):
                for c in (c0, c0 + 1):
                    norm2_transposed("last", 0, b, c)
                for c in (c0, c0 + 1):
                    feed("last", 0, c)

        @block.scalar
        def _(act):
            def misc(phase, it, name):
                bank, used = misc_use(phase, it, name)
                act.wait_ge(mi_full[bank], used + 1)
                return mi[bank], mi_free[bank]

            def split_high():
                act.wait_ge(w_loaded, 16 * 10)
                for d in range(2):
                    nc.scalar.activation(w_hi[:, d], raw_w[d][:, :, 0:DPROJ - NH], ACT.Copy).then_inc(wsplit_hi, 1)
                act.wait_ge(c_loaded, 16 * (2 + 2 * 8))
                act.wait_ge(setup_done, 1)
                nc.scalar.activation(wdt_hi[:], wdt, ACT.Copy).then_inc(wsplit_hi, 1)
                nc.scalar.activation(arow[:], arow[:], ACT.Exp).then_inc(a_exp, 1)

            def fold_weights():
                n = 0
                for d in range(2):
                    for t in range(KI):
                        ps, free = misc("weights", 0, n)
                        nc.scalar.activation(wc[:, d, t, :], ps[:, 0:D], ACT.Copy, scale=nw[:, d, t:t + 1]).then_inc(free, 1)
                        n += 1

            def norm_high(phase, it):
                for k in range(KD):
                    ps, _ = misc(phase, it, f"a{k}")
                    nc.scalar.activation(xnt_hi[:, k, :], ps[:], ACT.Copy).then_inc(xnt_hi_ready, 1)

            def dt_bias(phase, it):
                ps, free = misc(phase, it, "dtm")
                nc.scalar.activation(dt_t, ps[0:2 * NH, :], ACT.Identity, bias=dtb_sb[:, 0:1]).then_inc(free, 1)

            def softplus(b):
                act.wait_ge(na_ready, b + 1)
                nc.scalar.activation(e[:], na[:], ACT.Exp).then_inc(e_ready, 1)
                act.wait_ge(u_ready, b + 1)
                nc.scalar.activation(lnu[:], u1[:], ACT.Ln).then_inc(ln_ready, 1)

            def s_pieces(phase, it):
                ps, free = misc(phase, it, "ST")
                nc.scalar.activation(st_bf[:], ps[0:NS, 0:T // 2].bitcast(BF16), ACT.Copy).then_inc(free, 1)

            def conv_start(b, d, t):
                bank, used = pj_use(b, d, t)
                u = 2 * b + d
                if t == 0 and not (isinstance(b, int) and b == d == 0):
                    act.wait_ge(xs_ready, KI * u)
                elif t == 3:
                    act.wait_ge(bc_ready, u + 1)
                elif t == 4:
                    act.wait_ge(xs_ready, KI * u + 1)
                act.wait_ge(pj_full[bank], used + 1)
                nc.scalar.activation(xc[:, t % 3, :], pj[bank][:], ACT.Identity, bias=cb[:, d, t:t + 1],
                                     scale=cw[:, d, t, KW - 1:KW]).then_inc(conv_first, 1)

            def conv_end(b, d, t):
                bank, used = pj_use(b, d, t)
                act.wait_ge(pj_free[bank], used + 2)
                dst, ready = (bcm[:, d, :], bc_ready) if t == 0 else (xs[:, d, t - 1, :], xs_ready)
                nc.scalar.activation(dst, xc[:, t % 3, :], ACT.Silu).then_inc(ready, 1)

            def gate(b, d, t):
                bank, used = pj_use(b, d, t)
                act.wait_ge(pj_full[bank], used + 1)
                nc.scalar.activation(sz[:, d, t - NCONV, :], pj[bank][:], ACT.Silu).then_inc(pj_free[bank], 1)

            def project(b, d, between):
                conv_start(b, d, 0)
                between.get(0, lambda: None)()
                conv_start(b, d, 1)
                conv_end(b, d, 0)
                for t in range(2, NCONV):
                    between.get(t, lambda: None)()
                    conv_start(b, d, t)
                    conv_end(b, d, t - 1)
                conv_end(b, d, NCONV - 1)
                for t in range(NCONV, NT):
                    between.get(t, lambda: None)()
                    gate(b, d, t)

            def decays(b):
                act.wait_ge(wd_ready, b + 1)
                nc.scalar.activation(w_end[:], wd[:], ACT.Exp)
                nc.scalar.activation(e_end[:], s_all[:, NCH:2 * NCH], ACT.Exp).then_inc(w_ready, 1)

            def spread(b, d, name):
                u = 2 * b + d
                bank, used = sb_use(b, d, name)
                n = int(name[1])
                act.wait_ge(sb_full[bank], used + 1)
                if name[0] == "h":
                    act.wait_ge(m_ready, NH * u + n + 1)
                    for c in range(NC):
                        o = (d * NC + c) * NH + n
                        i = nc.scalar.activation(lx[:, n % 2, Q * c:Q * c + Q], sbk[bank][:, Q * c:Q * c + Q], ACT.Exp,
                                                 bias=neg_s[:, o:o + 1])
                    i.then_inc(sb_free[bank], 1)
                else:
                    act.wait_ge(c2_ready, KI * u + n + 1)
                    nc.scalar.activation(es[:, n % 2, :], sbk[bank][:], ACT.Exp).then_inc(sb_free[bank], 1)

            def b_tokens(phase, it, d):
                ps, free = misc(phase, it, f"{d}bt")
                src = ps[:, 0:NC * NS].rearrange("p (c n) -> p c n", c=NC)
                for half in range(2):
                    i = nc.scalar.activation(btok[:, :, half, :], src, ACT.Copy)
                i.then_inc(free, 1)

            def scan(phase, it, b, d, between):
                spread(b, d, "h0")
                spread(b, d, "h1")
                b_tokens(phase, it, d)
                for name in BC[2:9]:
                    spread(b, d, name)
                between()
                for name in BC[9:]:
                    spread(b, d, name)

            def norm2(phase, it, c):
                ps, free = misc(phase, it, f"t{c}")
                nc.scalar.activation(xn2t[:, c % 2], ps[:, 0:D].rearrange("p (k n) -> p k n", k=KD), ACT.Copy).then_inc(free, 1)

            split_high()
            fold_weights()
            norm_high("first", 0)
            project(0, 0, {})
            dt_bias("first", 0)
            project(0, 1, {0: lambda: softplus(0), NCONV: lambda: s_pieces("first", 0)})

            with act.Fori(0, NB - 1) as it:
                nxt = it + 1
                decays(it)
                scan("loop", it, it, 0, lambda: norm_high("loop", it))
                act.wait_ge(yg_ready, KI * (2 * it + 1))
                project(nxt, 0, {})
                scan("loop", it, it, 1, lambda: None)
                dt_bias("loop", it)
                act.wait_ge(yg_ready, KI * (2 * it + 2))

                def second_norm(c):
                    norm2("loop", it, c)
                    norm2("loop", it, c + 1)

                project(nxt, 1, {0: lambda: softplus(nxt), NCONV - 1: lambda: second_norm(0),
                                 NCONV: lambda: s_pieces("loop", it), NCONV + 1: lambda: second_norm(2)})

            b = NB - 1
            decays(b)
            scan("last", 0, b, 0, lambda: None)
            scan("last", 0, b, 1, lambda: None)
            for c in range(NC):
                norm2("last", 0, c)

        @block.vector
        def _(dve):
            for s in (*pj_free, *sb_free, *py_free, *mi_free):
                dve.sem_inc(s, 1)
            for s in (m_ready, c2_ready):
                dve.sem_inc(s, 2)
            dve.sem_inc(out_stored, 1)

            def misc(phase, it, name):
                bank, used = misc_use(phase, it, name)
                dve.wait_ge(mi_full[bank], used + 1)
                return mi[bank], mi_free[bank]

            def setup():
                dve.memset(wdt[:, :, 2 * NH:P], 0.0)
                dve.memset(halves[:], -0.5)
                dve.memset(spc[:], 0.0)
                dve.memset(hst[:], 0.0).then_inc(setup_done, 1)
                dve.wait_ge(c_loaded, 16 * (2 + 2 * 8))
                dve.tensor_copy(identb[:], ident)
                for d in range(2):
                    dve.tensor_scalar(hide[:, d, :], tri[d], -FAR, FAR, ALU.mult, ALU.add)
                dve.tensor_copy(sel[:], selc[:].unsqueeze(2).broadcast_to([NS, 2 * NH, P]))
                dve.tensor_copy(selp[:], selc[:].unsqueeze(2).broadcast_to([NS, 2 * NH, HP])).then_inc(sel_done, 1)

            def split_low():
                dve.wait_ge(w_loaded, 16 * 10)
                for d in range(2):
                    dve.wait_ge(wsplit_hi, d + 1)
                    dve.tensor_tensor(w_lo[:, d], raw_w[d][:, :, 0:DPROJ - NH], w_hi[:, d].bitcast(F32),
                                      ALU.subtract).then_inc(wsplit_lo, 1)
                dve.wait_ge(wsplit_hi, 3)
                dve.tensor_tensor(wdt_lo[:], wdt, wdt_hi[:].bitcast(F32), ALU.subtract).then_inc(wsplit_lo, 1)
                dve.wait_ge(a_exp, 1)
                dve.tensor_scalar(abc[:], arow[:].unsqueeze(1).broadcast_to([P, NC, 2 * NH]), -1.0, None,
                                  ALU.mult).then_inc(a_done, 1)

            def fold_ffn():
                for k in range(KD):
                    ps, free = misc("weights", 0, 2 * KI + k)
                    dve.tensor_tensor(wff[:, k, :], ps[:, 0:D], raw_ffT[:, k, :], ALU.add).then_inc(free, 1)

            def norm_stats(src, st, mv, stats, aggr, b):
                for c in range(NC):
                    dve.bn_stats(st[:, c, :], src[:, c, :]).then_inc(stats, 1)
                for c in range(NC):
                    dve.wait_ge(stats, NC * b + c + 1)
                    alone(dve)
                    dve.bn_aggr(mv[:, c, :], st[:, c, :]).then_inc(aggr, 1)

            def norm_scale(dst, src, mv, rstd, ready):
                for c in range(NC):
                    dve.tensor_scalar(dst[:, c, :], src[:, c, :], mv[:, c, 0:1], rstd[:, c:c + 1],
                                      ALU.subtract, ALU.mult).then_inc(ready, 1)

            def norm1_stats(b):
                dve.wait_ge(x_loaded, 16 * (b + 1))
                norm_stats(xin, st1, mv1, ln1_stats, ln1_mv, b)

            def norm1_scale(b):
                dve.wait_ge(ln1_rstd, b + 1)
                norm_scale(xn, xin, mv1, rstd1, xn_ready)

            def norm_low(phase, it, b):
                for k in range(KD):
                    ps, free = misc(phase, it, f"a{k}")
                    dve.wait_ge(xnt_hi_ready, KD * b + k + 1)
                    dve.tensor_tensor(xnt_lo[:, k, :], ps[:], xnt_hi[:, k, :].bitcast(F32), ALU.subtract).then_inc(free, 1)

            def soft_in(phase, it, b):
                ps, free = misc(phase, it, "dtt")
                dve.tensor_copy(v[:], ps[:, 0:NCH]).then_inc(free, 1)
                bank, used = misc_use(phase, it, "dtt")
                dve.wait_ge(free, used + 2)
                dve.scalar_tensor_tensor(na[:], v[:], -1.0, v[:], ALU.mult, ALU.min).then_inc(na_ready, 1)

            def soft_mid(b):
                dve.wait_ge(e_ready, b + 1)
                dve.tensor_scalar(u1[:], e[:], 1.0, None, ALU.add).then_inc(u_ready, 1)
                dve.wait_ge(u_ready, b + 1)
                dve.tensor_scalar(du[:], u1[:], -1.0, None, ALU.add).then_inc(dt_step, 1)
                dve.wait_ge(dt_step, 8 * b + 1)
                dve.scalar_tensor_tensor(dd[:], du[:], 0.0, du[:], ALU.is_equal, ALU.add).then_inc(dt_step, 1)
                dve.wait_ge(dt_step, 8 * b + 2)
                dve.reciprocal(rq[:], dd[:]).then_inc(dt_step, 1)

            def soft_out(b):
                dve.wait_ge(ln_ready, b + 1)
                dve.wait_ge(dt_step, 8 * b + 3)
                dve.tensor_tensor(r1[:], lnu[:], rq[:], ALU.mult).then_inc(dt_step, 1)
                dve.wait_ge(dt_step, 8 * b + 4)
                dve.scalar_tensor_tensor(r2[:], du[:], 0.0, r1[:], ALU.is_equal, ALU.add).then_inc(dt_step, 1)
                dve.wait_ge(dt_step, 8 * b + 5)
                dve.tensor_tensor(r3[:], r2[:], e[:], ALU.mult).then_inc(dt_step, 1)
                dve.wait_ge(dt_step, 8 * b + 6)
                dve.scalar_tensor_tensor(dt[:], v[:], 0.0, r3[:], ALU.max, ALU.add).then_inc(dt_step, 1)
                dve.wait_ge(dt_step, 8 * b + 7)
                dve.tensor_tensor(adt[:], dt[:], abc[:].rearrange("p c n -> p (c n)"), ALU.mult).then_inc(dt_step, 1)
                dve.wait_ge(dt_step, 8 * b + 8)
                dve.tensor_scalar(al[:], adt[:], A_FLOOR, None, ALU.max).then_inc(al_ready, 1)

            def s_values(phase, it, b):
                ps, free = misc(phase, it, "S")
                dve.tensor_copy(s_all[:], ps[:, 0:2 * NCH]).then_inc(free, 1)
                _, used = misc_use(phase, it, "S")
                dve.wait_ge(free, used + 2)
                dve.tensor_scalar(neg_s[:], s_all[:, 0:NCH], -1.0, None, ALU.mult).then_inc(s_ready, 1)
                dcn = "p (d c h) -> p d c h"
                for d in range(2):
                    i = dve.tensor_tensor(wd[:].rearrange(dcn, d=2, h=NH)[:, d],
                                          s_all[:, NCH:2 * NCH].rearrange("p (c d h) -> p d c h", d=2, h=NH)[:, d],
                                          s_all[:, 0:NCH].rearrange(dcn, d=2, h=NH)[:, d], ALU.subtract)
                i.then_inc(wd_ready, 1)

            def conv(b, d, t):
                u = 2 * b + d
                bank, used = pj_use(b, d, t)
                dve.wait_ge(conv_first, NCONV * u + t + 1)
                for s in range(1, KW):
                    to = slice(s, T) if d == 0 else slice(0, T - s)
                    of = slice(0, T - s) if d == 0 else slice(s, T)
                    if s > 1:
                        dve.wait_ge(conv_step, (KW - 2) * (NCONV * u + t) + s - 1)
                    i = dve.scalar_tensor_tensor(xc[:, t % 3, to], pj[bank][:, of], cw[:, d, t, KW - 1 - s:KW - s],
                                                 xc[:, t % 3, to], ALU.mult, ALU.add)
                    i.then_inc(pj_free[bank] if s == KW - 1 else conv_step, 1)

            def x_tokens(phase, it, d, j):
                ps, free = misc(phase, it, f"{d}x{j}")
                c = ORDER[d][j]
                o = 2 * NH * c + NH * d
                dve.tensor_tensor(xdt[:, c, :].rearrange("p (h q) -> p h q", h=NH), ps[:].rearrange("p (h q) -> p h q", h=NH),
                                  dt[:, o:o + NH].unsqueeze(2).broadcast_to([P, NH, HP]), ALU.mult).then_inc(free, 1)

            def scores(phase, it, b, d):
                ps, free = misc(phase, it, f"{d}g")
                dve.tensor_copy(gm[:], ps[:]).then_inc(free, 1)

            def weights(phase, it, b, d, h):
                u = 2 * b + d
                if h == 0:
                    bank, used = misc_use(phase, it, f"{d}g")
                    dve.wait_ge(mi_free[bank], used + 2)
                bank, used = sb_use(b, d, f"h{h}")
                dve.wait_ge(sb_free[bank], used + 2)
                dve.tensor_tensor(mx[:, h % 4, :], lx[:, h % 2, :], gm[:], ALU.mult).then_inc(m_ready, 1)

            def state(phase, it, b, d, j):
                u = 2 * b + d
                ps, free = misc(phase, it, f"{d}s{j}")
                if j:
                    dve.wait_ge(hs_ready, (NC - 2) * u + j)
                view = ps[:].rearrange("p (r e q) -> p r e q", e=2, q=HP)
                for half in range(2):
                    lanes, cols = slice(HP * half, HP * half + HP), slice(HP * half, HP * half + HP)
                    if j == 0:
                        i = dve.tensor_copy(hst[lanes, j, :, cols], view[lanes, :, half, :])
                    else:
                        i = dve.tensor_tensor(hst[lanes, j, :, cols], view[lanes, :, half, :], hs[lanes, :, cols], ALU.add)
                i.then_inc(free, 1)

            def outputs(b, d, p):
                u = 2 * b + d
                bank, used = py_use(b, d, p)
                if p:
                    dve.wait_ge(yg_ready, KI * u + p)
                dve.wait_ge(py_full[bank], used + 1)
                dve.scalar_tensor_tensor(yt[:], xs[:, d, p, :], dsk[:, d, p:p + 1], py[bank][:], ALU.mult,
                                         ALU.add).then_inc(py_free[bank], 1)
                dve.wait_ge(py_free[bank], used + 2)
                dve.tensor_tensor(yg[:, d, p, :], yt[:], sz[:, d, p, :], ALU.mult).then_inc(yg_ready, 1)

            def squares(phase, it, d):
                ps, free = misc(phase, it, f"{d}ss")
                dve.tensor_copy(ss[:, d, :], ps[:, 0:NC]).then_inc(free, 1)

            def mix(phase, it, b, c):
                ps, free = misc(phase, it, f"o{c}")
                if c == 0:
                    dve.wait_ge(xres_ready, b + 1)
                    dve.wait_ge(rms_ready, b + 1)
                dve.scalar_tensor_tensor(xres[:, c, :], ps[:, 0:D], rms[:, c:c + 1], xres[:, c, :], ALU.mult,
                                         ALU.add).then_inc(x1_step, 1)
                dve.wait_ge(x1_step, NC * b + c + 1)
                dve.scalar_tensor_tensor(xres[:, c, :], ps[:, D:2 * D], rms[:, NC + c:NC + c + 1], xres[:, c, :],
                                         ALU.mult, ALU.add).then_inc(free, 1)

            def norm2_stats(phase, it, b):
                for c in (NC - 2, NC - 1):
                    bank, used = misc_use(phase, it, f"o{c}")
                    dve.wait_ge(mi_free[bank], used + 2)
                norm_stats(xres, st2, mv2, ln2_stats, ln2_mv, b)

            def norm2_scale(b):
                dve.wait_ge(ln2_rstd, b + 1)
                norm_scale(xn2, xres, mv2, rstd2, xn2_ready)

            def feed(phase, it, b, c):
                ps, free = misc(phase, it, f"f{c}")
                if c == 0:
                    dve.wait_ge(otb_ready, b + 1)
                dve.tensor_tensor(ot[:, c, :], ps[:, 0:D], ot[:, c, :], ALU.add).then_inc(free, 1)

            def scan(phase, it, b, d, stats, scale, low):
                for j in range(NC):
                    x_tokens(phase, it, d, j)
                scores(phase, it, b, d)
                weights(phase, it, b, d, 0)
                weights(phase, it, b, d, 1)
                state(phase, it, b, d, 0)
                weights(phase, it, b, d, 2)
                stats()
                weights(phase, it, b, d, 3)
                state(phase, it, b, d, 1)
                state(phase, it, b, d, 2)
                scale()
                outputs(b, d, 0)
                weights(phase, it, b, d, 4)
                weights(phase, it, b, d, 5)
                outputs(b, d, 1)
                low()
                weights(phase, it, b, d, 6)
                weights(phase, it, b, d, 7)
                outputs(b, d, 2)
                outputs(b, d, 3)

            def nothing():
                pass

            setup()
            norm1_stats(0)
            norm1_scale(0)
            split_low()
            fold_ffn()
            norm_low("first", 0, 0)
            for t in range(NCONV):
                conv(0, 0, t)
            soft_in("first", 0, 0)
            conv(0, 1, 0)
            soft_mid(0)
            conv(0, 1, 1)
            soft_out(0)
            conv(0, 1, 2)
            s_values("first", 0, 0)
            conv(0, 1, 3)
            conv(0, 1, 4)

            with dve.Fori(0, NB - 1) as it:
                nxt = it + 1
                scan("loop", it, it, 0, lambda: norm1_stats(nxt), lambda: norm1_scale(nxt), lambda: norm_low("loop", it, nxt))
                for t in range(NCONV):
                    conv(nxt, 0, t)
                squares("loop", it, 0)
                scan("loop", it, it, 1, nothing, nothing, nothing)
                soft_in("loop", it, nxt)
                conv(nxt, 1, 0)
                soft_mid(nxt)
                conv(nxt, 1, 1)
                squares("loop", it, 1)
                mix("loop", it, it, 0)
                mix("loop", it, it, 1)
                soft_out(nxt)
                conv(nxt, 1, 2)
                mix("loop", it, it, 2)
                mix("loop", it, it, 3)
                s_values("loop", it, nxt)
                norm2_stats("loop", it, it)
                conv(nxt, 1, 3)
                norm2_scale(it)
                conv(nxt, 1, 4)
                for c in range(NC):
                    feed("loop", it, it, c)

            b = NB - 1
            scan("last", 0, b, 0, nothing, nothing, nothing)
            squares("last", 0, 0)
            scan("last", 0, b, 1, nothing, nothing, nothing)
            squares("last", 0, 1)
            for c in range(NC):
                mix("last", 0, b, c)
            norm2_stats("last", 0, b)
            norm2_scale(b)
            for c in range(NC):
                feed("last", 0, b, c)

        @block.gpsimd
        def _(pool):
            def keep_x(b):
                pool.wait_ge(x_loaded, 16 * (b + 1))
                pool.tensor_tensor(xres[:], xin[:], bo_sb[:].unsqueeze(1).broadcast_to([P, NC, D]), ALU.add).then_inc(xres_ready, 1)

            def inv_sqrt(src, mid, dst, scale, mid_ready, ready, b):
                alone(pool)
                pool.tensor_scalar(mid, src, scale, EPS, ALU.mult, ALU.add).then_inc(mid_ready, 1)
                pool.wait_ge(mid_ready, b + 1)
                n = mid.shape[-1]
                pool.tensor_tensor(dst, mid, halves[:, 0:n], ALU.pow).then_inc(ready, 1)

            def norm1(b):
                pool.wait_ge(ln1_mv, NC * (b + 1))
                inv_sqrt(mv1[:, :, 1], ve1[:], rstd1[:], 1.0, ln1_ve, ln1_rstd, b)

            def norm2(b):
                pool.wait_ge(ln2_mv, NC * (b + 1))
                inv_sqrt(mv2[:, :, 1], ve2[:], rstd2[:], 1.0, ln2_ve, ln2_rstd, b)

            def root_mean_square(phase, it, b):
                for d in range(2):
                    bank, used = misc_use(phase, it, f"{d}ss")
                    pool.wait_ge(mi_free[bank], used + 2)
                inv_sqrt(ss[:].rearrange("p d c -> p (d c)"), ms[:], rms[:], 1.0 / DI, ms_ready, rms_ready, b)

            def pieces(b):
                pool.wait_ge(s_ready, b + 1)
                dch = "p (d c h) -> p d c h"
                left = s_all[:, 0:NCH].rearrange(dch, d=2, h=NH)
                rest = [rem1[:].rearrange(dch, d=2, h=NH), rem2[:].rearrange(dch, d=2, h=NH)]
                view = spc[:].rearrange("p c (d r) -> p d c r", d=2)
                steps = 4 * PIECES - 2
                n = 0
                for q in range(PIECES):
                    alone(pool)
                    for d in range(2):
                        i = pool.tensor_copy(view[:, d, :, NH * q:NH * q + NH], left[:, d])
                        i.then_inc(spc_ready if (q, d) == (PIECES - 1, 1) else spc_step, 1)
                        n += 1
                    if q < PIECES - 1:
                        pool.wait_ge(spc_step, (steps - 1) * b + n)
                        for d in range(2):
                            pool.tensor_tensor(rest[q][:, d], left[:, d], view[:, d, :, NH * q:NH * q + NH],
                                               ALU.subtract).then_inc(spc_step, 1)
                            n += 1
                        pool.wait_ge(spc_step, (steps - 1) * b + n)
                        left = rest[q]

            def decayed_x(phase, it, b, d, j):
                if j == 0:
                    pool.wait_ge(w_ready, b + 1)
                bank, used = misc_use(phase, it, f"{d}x{j}")
                pool.wait_ge(mi_free[bank], used + 2)
                c = ORDER[d][j]
                o = (d * NC + c) * NH
                hq = "p (h q) -> p h q"
                pool.tensor_tensor(xw[:, j, :].rearrange(hq, h=NH), xdt[:, c, :].rearrange(hq, h=NH),
                                   w_end[:, o:o + NH].unsqueeze(2).broadcast_to([P, NH, HP]), ALU.mult).then_inc(xw_ready, 1)

            def decayed_c(b, d, p):
                bank, used = sb_use(b, d, f"p{p}")
                pool.wait_ge(sb_free[bank], used + 2)
                if p >= 2:
                    bank, used = py_use(b, d, p - 2)
                    pool.wait_ge(py_full[bank], used + 1)
                pool.tensor_tensor(c2[:, p % 2, :], cc[:, d, :], es[:, p % 2, :], ALU.mult).then_inc(c2_ready, 1)

            def decayed_state(phase, it, b, d, j):
                bank, used = misc_use(phase, it, f"{d}s{j - 1}")
                pool.wait_ge(mi_free[bank], used + 2)
                o = (2 * ORDER[d][j] + d) * NH
                pool.tensor_tensor(hs[:].rearrange("p r (e q) -> p (r e) q", e=2),
                                   hst[:, j - 1].rearrange("p r (e q) -> p (r e) q", e=2),
                                   e_end[:, o:o + NH].unsqueeze(2).broadcast_to([P, NH, HP]), ALU.mult).then_inc(hs_ready, 1)

            def squares(b, d):
                u = 2 * b + d
                n = 2 * KI - 2
                for t in range(KI):
                    pool.wait_ge(yg_ready, KI * u + t + 1)
                    if t >= 2:
                        pool.wait_ge(sq_step, n * u + 2 * t - 1)
                    to = sqsum if t == 0 else sq
                    pool.tensor_tensor(to[:], yg[:, d, t, :], yg[:, d, t, :], ALU.mult).then_inc(sq_step, 1)
                    if t:
                        pool.wait_ge(sq_step, n * u + 2 * t)
                        i = pool.tensor_tensor(sqsum[:], sqsum[:], sq[:], ALU.add)
                        i.then_inc(sqsum_ready if t == KI - 1 else sq_step, 1)

            def scan(phase, it, b, d, between):
                decayed_x(phase, it, b, d, 0)
                decayed_x(phase, it, b, d, 1)
                decayed_x(phase, it, b, d, 2)
                decayed_c(b, d, 0)
                decayed_state(phase, it, b, d, 1)
                decayed_c(b, d, 1)
                decayed_state(phase, it, b, d, 2)
                between()
                decayed_c(b, d, 2)
                decayed_c(b, d, 3)
                squares(b, d)

            def result_bias(phase, it, b):
                bank, used = misc_use(phase, it, f"o{NC - 1}")
                pool.wait_ge(mi_free[bank], used + 2)
                pool.wait_ge(out_stored, 16 * NC * b + 1)
                pool.tensor_tensor(ot[:], xres[:], ffb_sb[:].unsqueeze(1).broadcast_to([P, NC, D]), ALU.add).then_inc(otb_ready, 1)

            pool.wait_ge(setup_done, 1)
            norm1(0)
            pool.wait_ge(w_loaded, 16 * 10)
            keep_x(0)
            pieces(0)

            with pool.Fori(0, NB - 1) as it:
                nxt = it + 1
                scan("loop", it, it, 0, lambda: norm1(nxt))
                scan("loop", it, it, 1, lambda: None)
                root_mean_square("loop", it, it)
                norm2(it)
                result_bias("loop", it, it)
                pieces(nxt)
                pool.wait_ge(xn2_ready, NC * (it + 1))
                keep_x(nxt)

            b = NB - 1
            scan("last", 0, b, 0, lambda: None)
            scan("last", 0, b, 1, lambda: None)
            root_mean_square("last", 0, b)
            norm2(b)
            result_bias("last", 0, b)


_DIRS = ("f", "b")
_OUT = ((NB, T, D), "float32")


def _arrays(inputs):
    import numpy as np

    def get(name):
        return np.ascontiguousarray(inputs["L0_" + name])

    tok = np.arange(P)
    consts = np.zeros((P, 4, P), np.float32)
    consts[:, 0] = np.eye(P)
    consts[:, 1] = tok[:, None] <= tok[None, :]
    consts[:, 2] = tok[:, None] >= tok[None, :]
    consts[:, 3] = 1.0
    selcol = np.zeros((NS, 2 * NH), np.float32)
    for d in range(2):
        for q in range(PIECES):
            for h in range(NH):
                selcol[NS // 2 * d + NH * q + h, NH * d + h] = 1.0

    tiles = [KI] + list(range(KI))
    arrays = {"x": get("attn_x"), "consts": consts, "selcol": selcol}
    for s in _DIRS:
        arrays[s + "win"] = get(f"attn_{s}Win")
        arrays[s + "convw"] = get(f"attn_{s}convw").reshape(KW, NCONV, P).transpose(2, 1, 0)[:, tiles]
        arrays[s + "convb"] = get(f"attn_{s}convb").reshape(NCONV, P).transpose(1, 0)[:, tiles]
        arrays[s + "dtb"] = get(f"attn_{s}dtb")
        arrays[s + "alog"] = get(f"attn_{s}Alog")
        arrays[s + "dskip"] = get(f"attn_{s}D").reshape(KI, 2).transpose(1, 0)
        arrays[s + "normw"] = get(f"attn_{s}normw").reshape(KI, P).transpose(1, 0)
        arrays[s + "woutT"] = get(f"attn_{s}Wout").transpose(1, 0)
    arrays |= {"wo": get("attn_Wo"), "bo": get("attn_bo"), "ffT": get("ffn_W").transpose(1, 0), "ffb": get("ffn_b"),
               "vrT": get("ffn_V_r").transpose(1, 0), "cT": get("ffn_C").transpose(1, 0)}
    return {k: np.ascontiguousarray(v) for k, v in arrays.items()}


def kernel(**inputs):
    import numpy as np
    import concourse.bacc as bacc
    from concourse.bass_utils import run_bass_kernel_spmd

    nc = bacc.Bacc("TRN2", target_bir_lowering=False, num_devices=1)
    arrays = {f"in_{k}": v for k, v in _arrays(inputs).items()}
    ap = {k[3:]: nc.dram_tensor(k, v.shape, mybir.dt.from_np(v.dtype), kind="ExternalInput").ap() for k, v in arrays.items()}
    out = nc.dram_tensor("out", _OUT[0], mybir.dt.from_np(np.dtype(_OUT[1])), kind="ExternalOutput").ap()

    def both(name):
        return [ap[s + name] for s in _DIRS]

    build(nc, ap["x"], ap["consts"], ap["selcol"], both("win"), both("convw"), both("convb"), both("dtb"), both("alog"),
          both("dskip"), both("normw"), both("woutT"), ap["wo"], ap["bo"], ap["ffT"], ap["ffb"], ap["vrT"], ap["cT"], out)
    result = run_bass_kernel_spmd(nc, [arrays], core_ids=[0])
    return result.results[0]["out"]
```

```python
from contextlib import ExitStack

import concourse.bass as bass
from concourse import mybir

F32 = mybir.dt.float32
F32R = mybir.dt.float32r
BF16 = mybir.dt.bfloat16
ALU = mybir.AluOpType
ACT = mybir.ActivationFunctionType

P = 128
NB, T, D = 8, 512, 256
DI, NS, NH, HP = 512, 64, 8, 64
KW = 4
DPROJ = 2 * DI + 2 * NS + NH
Q = 128
NC = T // Q
KD = D // P
KI = DI // P
RANK = 32
EPS = 1e-5
A_FLOOR = -105.0
FAR = -32768.0
PIECES = 3

COLS = [2 * DI] + [DI + P * t for t in range(KI)] + [P * t for t in range(KI)]
NCONV = 1 + KI
NT = len(COLS)

ORDER = [list(range(NC)), list(reversed(range(NC)))]
BC = ["h0", "h1", "p0", "h2", "h3", "p1", "h4", "h5", "p2", "h6", "h7", "p3"]

WEIGHTS = [f"w{n}" for n in range(2 * KI + 1)]
TOK0, TOK1 = ([f"{d}{n}" for n in ("bt", "x0", "x1", "x2", "x3", "g", "s0", "s1")] for d in range(2))
FFN = ["t0", "t1", "f0", "f1", "t2", "t3", "f2", "f3"]
START = ["a0", "a1", "dtm", "dtt", "0S"] + WEIGHTS[0:KI] + ["0ST"] + WEIGHTS[KI:] + TOK0 + ["0s2", "1S", "1ST"]
LOOP = (TOK1 + ["0ss", "a0", "a1", "1s2", "0o0", "dtm", "0o1", "dtt", "0S", "0ST"]
        + TOK0 + ["1ss", "0s2", "1S", "1o0", "1o1", "1ST"] + FFN)
LAST = TOK1 + ["0ss", "1s2", "0o0", "0o1", "1ss", "1o0", "1o1"] + FFN
assert len(START) % 2 == 0 and len(LOOP) % 2 == 0


def misc_use(phase, it, name):
    if phase == "start":
        n = START.index(name)
        return n % 2, n // 2
    if phase == "loop":
        n = len(START) + LOOP.index(name)
        return n % 2, it * (len(LOOP) // 2) + n // 2
    n = len(START) + (NB - 1) * len(LOOP) + LAST.index(name)
    return n % 2, n // 2


def build(nc, x, consts, selcol, win, convw, convb, dtb, alog, dskip, normw, woutT, wo, bo, ffT, ffb, vrT, cT, out):
    with ExitStack() as ctx:
        def sb(name, shape, dt=F32):
            return ctx.enter_context(nc.sbuf_tensor(name, shape, dt))

        def sem(name):
            return ctx.enter_context(nc.semaphore(name))

        cst = sb("cst", [P, 4, P])
        ident, upto, since, ones = (cst[:, i, :] for i in range(4))
        tri = [upto, since]
        identb = sb("identb", [P, P], BF16)
        selc = sb("selc", [P, NH])
        sel = sb("sel", [P, NH, P], BF16)
        selp = sb("selp", [P, NH, HP], BF16)
        hide = sb("hide", [P, 2, Q], BF16)
        halves = sb("halves", [P, 16])
        w_hi = sb("w_hi", [P, 2, KD, DPROJ - NH], F32R)
        w_lo = sb("w_lo", [P, 2, KD, DPROJ - NH], F32R)
        wdt_hi = sb("wdt_hi", [P, KD, P], F32R)
        wdt_lo = sb("wdt_lo", [P, KD, P], F32R)
        cw = sb("cw", [P, 2, NCONV, KW])
        cb = sb("cb", [P, 2, NCONV])
        dtb_sb = sb("dtb_sb", [2 * NH, 1])
        arow = sb("arow", [P, 2 * NH])
        abc = sb("abc", [P, NC, 2 * NH])
        dsk = sb("dsk", [P, 2, KI])
        nw = sb("nw", [P, 2, KI])
        wc = sb("wc", [P, 2, KI, D])
        wff = sb("wff", [P, KD, D])
        bo_sb = sb("bo_sb", [P, D])
        ffb_sb = sb("ffb_sb", [P, D])

        xin = sb("xin", [P, NC, D])
        xres = sb("xres", [P, NC, D])
        st1 = sb("st1", [P, NC, 6])
        mv1 = sb("mv1", [P, NC, 2])
        ve1 = sb("ve1", [P, NC])
        rstd1 = sb("rstd1", [P, NC])
        xn = sb("xn", [P, NC, D])
        xnt_hi = sb("xnt_hi", [P, KD, T], F32R)
        xnt_lo = sb("xnt_lo", [P, KD, T], F32R)
        NCH = NC * NH
        v, na, e, u1, du, dd, rq, r2, r3 = (sb(n, [P, NC, 2 * NH]) for n in "v na e u1 du dd rq r2 r3".split())
        lnu, r1 = na, dd
        rem1 = sb("rem1", [P, NC, NH])
        rem2 = sb("rem2", [P, NC, NH])
        spc = sb("spc", [P, NC, P], BF16)
        ss = sb("ss", [P, 2, NC])
        ms = sb("ms", [P, 2, NC])
        rms = sb("rms", [P, 2, NC])
        st2 = sb("st2", [P, NC, 6])
        mv2 = sb("mv2", [P, NC, 2])
        ve2 = sb("ve2", [P, NC])
        rstd2 = sb("rstd2", [P, NC])
        xn2 = xn
        xn2t = sb("xn2t", [P, 2, KD, P])
        ot = sb("ot", [P, NC, D])
        dt_t = ot[0:2 * NH, 0:2, :].rearrange("p c n -> p (c n)")

        dt, adt, al = (sb(n, [P, 2, NC, NH]) for n in "dt adt al".split())
        s_all = sb("s_all", [P, 2, 2, NC, NH])
        neg_s = sb("neg_s", [P, 2, NCH])
        wd = sb("wd", [P, 2, NCH])
        w_end = sb("w_end", [P, 2, NCH])
        e_end = sb("e_end", [P, 2, NCH])
        st_bf = sb("st_bf", [P, 2, T], BF16)
        xc = sb("xc", [P, NCONV, T])
        xs = sb("xs", [P, 2, KI, T])
        bcm = sb("bcm", [P, 2, T])
        cc = sb("cc", [P, 2, T])
        cz = sb("cz", [P, T])
        sz = sb("sz", [P, 2, KI, T])
        xdt = sb("xdt", [P, NC, DI])
        xw = sb("xw", [P, NC - 1, DI])
        btok = sb("btok", [P, NC, NS])
        gm = sb("gm", [P, T])
        lx = sb("lx", [P, 2, T])
        mx = sb("mx", [P, 4, T])
        es = sb("es", [P, 2, T])
        c2 = sb("c2", [P, 2, T])
        hst = sb("hst", [P, NC - 1, KI, P])
        hs = sb("hs", [P, KI, P])
        yg = sb("yg", [P, 2, KI, T])
        sq = sb("sq", [P, T])
        sqsum = sb("sqsum", [P, T])

        flat = "p a t -> p (a t)"
        NW = DPROJ - NH
        raw_w = [[yg[:, 0].rearrange(flat)[:, 0:NW], yg[:, 1].rearrange(flat)[:, 0:NW]],
                 [xs[:, 1].rearrange(flat)[:, 0:NW], sz[:, 1].rearrange(flat)[:, 0:NW]]]
        wdt = hs[:, 0:KD, :]
        raw_woutT = xdt[:].rearrange("p c (k n) -> p c k n", k=1)[:, :, 0, :]
        raw_wo = xw[:].rearrange("p c n -> p (c n)")[:, 0:4 * D].rearrange("p (m n) -> p m n", m=4)
        raw_ffT = mx[:].rearrange("p c n -> p (c n)")[:, 0:KD * D].rearrange("p (k n) -> p k n", k=KD)
        raw_vrT = mx[0:RANK, 2, 0:D]
        raw_cT = mx[0:RANK, 2, D:2 * D]

        def banks(name, n):
            return [ctx.enter_context(nc.psum_tensor(f"{name}{i}", [P, T], F32)) for i in range(n)]

        pj, sbk, py, mi = banks("pj", 2), banks("sbk", 2), banks("py", 2), banks("mi", 2)

        def ring(name):
            return [sem(f"{name}_full{i}") for i in range(2)], [sem(f"{name}_free{i}") for i in range(2)]

        pj_full, pj_free = ring("pj")
        sb_full, sb_free = ring("sb")
        py_full, py_free = ring("py")
        mi_full, mi_free = ring("mi")

        (passed, c_loaded, v_loaded, f_loaded, setup_done, sel_done, wdt_hi_ready, wdt_lo_ready, a_exp, a_done, x_loaded,
         ln1_stats, ln1_mv, ln1_ve, ln1_rstd, xn_ready, xnt_hi_ready, xres_ready, na_ready, e_ready, u_ready, ln_ready,
         dt_step, r_ready, fin_step, al_ready, s_ready, wd_ready, w_ready, spc_step, spc_ready, conv_first,
         conv_step, bc_ready, xs_ready, xw_ready, m_ready, c2_ready, hs_ready, yg_ready, sq_step,
         sqsum_ready, ms_ready, rms_ready, x1_step, ln2_stats, ln2_mv, ln2_ve, ln2_rstd, xn2_ready,
         otb_ready, out_stored) = (sem(n) for n in (
            "passed c_loaded v_loaded f_loaded setup_done sel_done wdt_hi_ready wdt_lo_ready a_exp a_done x_loaded "
            "ln1_stats ln1_mv ln1_ve ln1_rstd xn_ready xnt_hi_ready xres_ready na_ready e_ready u_ready ln_ready "
            "dt_step r_ready fin_step al_ready s_ready wd_ready w_ready spc_step spc_ready conv_first conv_step bc_ready "
            "xs_ready xw_ready m_ready c2_ready hs_ready yg_ready sq_step sqsum_ready ms_ready rms_ready x1_step "
            "ln2_stats ln2_mv ln2_ve ln2_rstd xn2_ready otb_ready out_stored").split())

        w_loaded = [sem("w_loaded_f"), sem("w_loaded_b")]
        w_hi_ready = [sem("w_hi_ready_f"), sem("w_hi_ready_b")]
        w_lo_ready = [sem("w_lo_ready_f"), sem("w_lo_ready_b")]
        cc_loaded = [sem("cc_loaded_f"), sem("cc_loaded_b")]

        def pj_use(b, d, t):
            n = NT * d + t
            return n % 2, b * NT + n // 2

        def sb_use(b, d, name):
            n = len(BC) * d + BC.index(name)
            return n % 2, b * len(BC) + n // 2

        def py_use(b, d, p):
            n = KI * d + p
            return n % 2, b * KI + n // 2

        def alone(eng):
            eng.sem_inc(passed, 1)

        block = ctx.enter_context(nc.Block())

        @block.sync
        def _(sp):
            def load_win(d):
                for k in range(KD):
                    sp.dma_start(raw_w[d][k], win[d][P * k:P * k + P, 0:NW]).then_inc(w_loaded[d], 16)

            sp.dma_start(xin[:], x[0].rearrange("(c p) d -> p c d", p=P)).then_inc(x_loaded, 16)
            sp.dma_start(cst[:], consts).then_inc(c_loaded, 16)
            load_win(0)
            for d in range(2):
                sp.dma_start(wdt[:, :, NH * d:NH * d + NH],
                             win[d][:, NW:DPROJ].rearrange("(k p) n -> p k n", p=P)).then_inc(c_loaded, 16)
            sp.dma_start(selc[:], selcol).then_inc(c_loaded, 16)
            for d in range(2):
                sp.dma_start(cw[:, d], convw[d]).then_inc(v_loaded, 16)
                sp.dma_start(cb[:, d], convb[d]).then_inc(v_loaded, 16)
                sp.dma_start(dtb_sb[NH * d:NH * d + NH, :], dtb[d].rearrange("(h o) -> h o", o=1)).then_inc(v_loaded, 16)
                sp.dma_start(arow[:, NH * d:NH * d + NH], alog[d].partition_broadcast(P)).then_inc(v_loaded, 16)
            load_win(1)
            for d in range(2):
                sp.dma_start(nw[:, d], normw[d]).then_inc(f_loaded, 16)
                for e2 in range(2):
                    sp.dma_start(dsk[HP * e2:HP * e2 + HP, d, :],
                                 dskip[d][e2].partition_broadcast(HP)).then_inc(f_loaded, 16)
                sp.dma_start(raw_woutT[:, 2 * d:2 * d + 2, :],
                             woutT[d].rearrange("(m p) n -> p m n", p=P)).then_inc(f_loaded, 16)
            sp.dma_start(raw_wo, wo.rearrange("(m p) n -> p m n", p=P)).then_inc(f_loaded, 16)
            sp.dma_start(raw_ffT, ffT.rearrange("(k p) n -> p k n", p=P)).then_inc(f_loaded, 16)
            sp.dma_start(raw_vrT, vrT).then_inc(f_loaded, 16)
            sp.dma_start(raw_cT, cT).then_inc(f_loaded, 16)
            sp.dma_start(bo_sb[:], bo.partition_broadcast(P)).then_inc(f_loaded, 16)
            sp.dma_start(ffb_sb[:], ffb.partition_broadcast(P)).then_inc(f_loaded, 16)

            def copy_c(b, d):
                sp.wait_ge(bc_ready, 2 * b + d + 1)
                for dst in (cc[0:NS, d, :], cc[NS:P, d, :], cz[0:NS, :]):
                    sp.dma_start(dst, bcm[NS:P, d, :]).then_inc(cc_loaded[d], 16)

            def store(phase, it, b, c):
                bank, used = misc_use(phase, it, f"f{c}")
                sp.wait_ge(mi_free[bank], used + 2)
                alone(sp)
                sp.dma_start(out[b, Q * c:Q * c + Q, :], ot[:, c, :]).then_inc(out_stored, 16)

            copy_c(0, 0)
            copy_c(0, 1)
            with sp.Fori(0, NB - 1) as it:
                sp.wait_ge(xres_ready, it + 1)
                alone(sp)
                sp.dma_start(xin[:], x[it + 1].rearrange("(c p) d -> p c d", p=P)).then_inc(x_loaded, 16)
                copy_c(it + 1, 0)
                store("loop", it, it, 0)
                store("loop", it, it, 1)
                copy_c(it + 1, 1)
                store("loop", it, it, 2)
                store("loop", it, it, 3)
            for c in range(NC):
                store("last", 0, NB - 1, c)
            sp.wait_ge(out_stored, 16 * NC * NB + 1)

        @block.tensor
        def _(pe):
            def misc(phase, it, name):
                bank, used = misc_use(phase, it, name)
                pe.wait_ge(mi_free[bank], used + 1)
                return mi[bank], mi_full[bank]

            def fold_weights(uses):
                for n in uses:
                    ps, full = misc("start", 0, f"w{n}")
                    if n < 2 * KI:
                        d, t = divmod(n, KI)
                        for m in range(KD):
                            mm = pe.matmul(ps[:, 0:D], raw_woutT[:, 2 * d + m, P * t:P * t + P], raw_wo[:, 2 * d + m, :],
                                           start=(m == 0), stop=(m == KD - 1))
                    else:
                        for k in range(KD):
                            mm = pe.matmul(ps[:, D * k:D * k + D], raw_vrT[:, P * k:P * k + P], raw_cT, start=True, stop=True)
                    mm.then_inc(full, 1)

            def norm_transposed(phase, it, b):
                pe.wait_ge(xn_ready, NC * b + NC)
                for k in range(KD):
                    ps, full = misc(phase, it, f"a{k}")
                    for c in range(NC):
                        mm = pe.transpose(ps[:, Q * c:Q * c + Q], xn[:, c, P * k:P * k + P], ident)
                    mm.then_inc(full, 1)

            def released(phase, it, name):
                bank, used = misc_use(phase, it, name)
                pe.wait_ge(mi_free[bank], used + 2)

            def wait_xnt(phase, it):
                for k in range(KD):
                    released(phase, it, f"a{k}")

            def three_passes(ps, hi, lo):
                for k in range(KD):
                    pe.matmul(ps[:], hi(k), xnt_hi[:, k, :], start=(k == 0), stop=False)
                    pe.matmul(ps[:], hi(k), xnt_lo[:, k, :], start=False, stop=False)
                    mm = pe.matmul(ps[:], lo(k), xnt_hi[:, k, :], start=False, stop=(k == KD - 1))
                return mm

            def project(b, d, t):
                bank, used = pj_use(b, d, t)
                pe.wait_ge(pj_free[bank], used + 1)
                c0 = COLS[t]
                three_passes(pj[bank], lambda k: w_hi[:, d, k, c0:c0 + P],
                             lambda k: w_lo[:, d, k, c0:c0 + P]).then_inc(pj_full[bank], 1)

            def dt_project(phase, it):
                ps, full = misc(phase, it, "dtm")
                three_passes(ps, lambda k: wdt_hi[:, k, :], lambda k: wdt_lo[:, k, :]).then_inc(full, 1)

            def dt_transposed(phase, it):
                released(phase, it, "dtm")
                ps, full = misc(phase, it, "dtt")
                alone(pe)
                for c in range(NC):
                    mm = pe.transpose(ps[:, 2 * NH * c:2 * NH * (c + 1)], dt_t[:, Q * c:Q * c + Q], ident[0:2 * NH, 0:2 * NH])
                mm.then_inc(full, 1)

            def sums(phase, it, b, d):
                pe.wait_ge(al_ready, 2 * b + d + 1)
                ps, full = misc(phase, it, f"{d}S")
                av = al[:, d].rearrange("p c h -> p (c h)")
                pe.matmul(ps[:, 0:NCH], tri[d], av, start=True, stop=True)
                pe.matmul(ps[:, NCH:2 * NCH], ones, av, start=True, stop=True).then_inc(full, 1)

            def s_transposed(phase, it, b, d):
                pe.wait_ge(spc_ready, 2 * b + d + 1)
                ps, full = misc(phase, it, f"{d}ST")
                alone(pe)
                pb = ps[:, 0:T // 2].bitcast(BF16)
                for c in range(NC):
                    mm = pe.transpose(pb[:, Q * c:Q * c + Q], spc[:, c, :], identb[:])
                mm.then_inc(full, 1)

            def spread(b, d, name):
                bank, used = sb_use(b, d, name)
                pe.wait_ge(sb_free[bank], used + 1)
                n = int(name[1])
                w = sel[:, n, :] if name[0] == "h" else selp[:, 2 * n:2 * n + 2, :]
                mm = pe.matmul(sbk[bank][:], w, st_bf[:, d, :], start=True, stop=(name[0] == "p"))
                if name[0] == "h":
                    mm = pe.matmul(sbk[bank][:], identb[:], hide[:, d, :].unsqueeze(1).broadcast_to([P, NC, Q]),
                                   start=False, stop=True)
                mm.then_inc(sb_full[bank], 1)

            def b_tokens(phase, it, d):
                ps, full = misc(phase, it, f"{d}bt")
                for c in range(NC):
                    mm = pe.transpose(ps[:, P * c:P * c + P], bcm[:, d, Q * c:Q * c + Q], ident)
                mm.then_inc(full, 1)

            def x_tokens(phase, it, d, j):
                ps, full = misc(phase, it, f"{d}x{j}")
                c = ORDER[d][j]
                for t in range(KI):
                    mm = pe.transpose(ps[:, P * t:P * t + P], xs[:, d, t, Q * c:Q * c + Q], ident)
                mm.then_inc(full, 1)

            def scores(phase, it, b, d):
                pe.wait_ge(cc_loaded[d], 48 * (b + 1))
                ps, full = misc(phase, it, f"{d}g")
                for c in range(NC):
                    mm = pe.matmul(ps[:, Q * c:Q * c + Q], bcm[:, d, Q * c:Q * c + Q], cz[:, Q * c:Q * c + Q],
                                   start=True, stop=True)
                mm.then_inc(full, 1)

            def state(phase, it, b, d, j):
                u = 2 * b + d
                if j == 0:
                    released(phase, it, f"{d}bt")
                pe.wait_ge(xw_ready, (NC - 1) * u + j + 1)
                ps, full = misc(phase, it, f"{d}s{j}")
                heads = xw[:, j, :].rearrange("p (r e q) -> p e r q", e=2, q=HP)
                for half in range(2):
                    mm = pe.matmul(ps[NS * half:NS * half + NS, 0:DI // 2].rearrange("p (r q) -> p r q", q=HP),
                                   btok[:, ORDER[d][j], :], heads[:, half], start=True, stop=True, skip_group_check=True)
                mm.then_inc(full, 1)

            def outputs(phase, it, b, d, p):
                u = 2 * b + d
                bank, used = py_use(b, d, p)
                pe.wait_ge(py_free[bank], used + 1)
                pe.wait_ge(m_ready, 2 + NH * u + 2 * p + 2)
                for c in range(NC):
                    for half in range(2):
                        h = 2 * p + half
                        pe.matmul(py[bank][HP * half:HP * half + HP, Q * c:Q * c + Q], xdt[:, c, HP * h:HP * h + HP],
                                  mx[:, h % 4, Q * c:Q * c + Q], start=(c == 0), stop=False, skip_group_check=True)
                if p == 0:
                    released(phase, it, f"{d}s{NC - 2}")
                pe.wait_ge(c2_ready, 2 + KI * u + p + 1)
                for j in range(NC - 1):
                    c = ORDER[d][j + 1]
                    mm = pe.matmul(py[bank][:, Q * c:Q * c + Q], hst[:, j, p, :], c2[:, p % 2, Q * c:Q * c + Q],
                                   start=False, stop=(j == NC - 2), skip_group_check=True)
                mm.then_inc(py_full[bank], 1)

            def squares(phase, it, b, d):
                pe.wait_ge(sqsum_ready, 2 * b + d + 1)
                ps, full = misc(phase, it, f"{d}ss")
                for c in range(NC):
                    mm = pe.matmul(ps[:, c:c + 1], sqsum[:, Q * c:Q * c + Q], ones[:, 0:1], start=True, stop=True)
                mm.then_inc(full, 1)

            def mix(phase, it, b, d, half):
                if half == 0:
                    pe.wait_ge(yg_ready, KI * (2 * b + d + 1))
                ps, full = misc(phase, it, f"{d}o{half}")
                for i in range(2):
                    c = 2 * half + i
                    for t in range(KI):
                        mm = pe.matmul(ps[:, D * i:D * i + D], yg[:, d, t, Q * c:Q * c + Q], wc[:, d, t, :],
                                       start=(t == 0), stop=(t == KI - 1))
                mm.then_inc(full, 1)

            def norm2_transposed(phase, it, b, c):
                pe.wait_ge(xn2_ready, NC * b + c + 1)
                ps, full = misc(phase, it, f"t{c}")
                for k in range(KD):
                    mm = pe.transpose(ps[:, P * k:P * k + P], xn2[:, c, P * k:P * k + P], ident)
                mm.then_inc(full, 1)

            def feed(phase, it, c):
                released(phase, it, f"t{c}")
                ps, full = misc(phase, it, f"f{c}")
                for k in range(KD):
                    mm = pe.matmul(ps[:, 0:D], xn2t[:, c % 2, k, :], wff[:, k, :], start=(k == 0), stop=(k == KD - 1))
                mm.then_inc(full, 1)

            def scan_start(phase, it, b, d):
                pe.wait_ge(bc_ready, 2 * b + d + 1)
                b_tokens(phase, it, d)
                pe.wait_ge(xs_ready, KI * (2 * b + d + 1))
                x_tokens(phase, it, d, 0)
                x_tokens(phase, it, d, 1)
                project(b, d, NT - 2)
                x_tokens(phase, it, d, 2)
                x_tokens(phase, it, d, 3)
                project(b, d, NT - 1)
                if d == 0:
                    released(phase, it, "0ST")
                spread(b, d, "h0")
                spread(b, d, "h1")
                scores(phase, it, b, d)
                spread(b, d, "p0")

            def reversed_scan(phase, it, b, nxt):
                more = phase == "loop"
                scan_start(phase, it, b, 1)
                spread(b, 1, "h2")
                state(phase, it, b, 1, 0)
                spread(b, 1, "h3")
                state(phase, it, b, 1, 1)
                squares(phase, it, b, 0)
                spread(b, 1, "p1")
                if more:
                    norm_transposed(phase, it, nxt)
                spread(b, 1, "h4")
                state(phase, it, b, 1, 2)
                mix(phase, it, b, 0, 0)
                if more:
                    wait_xnt(phase, it)
                    dt_project(phase, it)
                    project(nxt, 0, 0)
                outputs(phase, it, b, 1, 0)
                mix(phase, it, b, 0, 1)
                spread(b, 1, "h5")
                spread(b, 1, "p2")
                if more:
                    project(nxt, 0, 1)
                    dt_transposed(phase, it)
                outputs(phase, it, b, 1, 1)
                spread(b, 1, "h6")
                spread(b, 1, "h7")
                if more:
                    project(nxt, 0, 2)
                spread(b, 1, "p3")
                outputs(phase, it, b, 1, 2)
                if more:
                    project(nxt, 0, 3)
                    project(nxt, 0, 4)
                outputs(phase, it, b, 1, 3)
                if more:
                    project(nxt, 0, 5)
                    sums(phase, it, nxt, 0)
                    project(nxt, 0, 6)
                    s_transposed(phase, it, nxt, 0)

            def forward_scan(phase, it, b, last):
                more = phase == "loop"
                scan_start(phase, it, b, 0)
                project(b, 1, 0)
                spread(b, 0, "h2")
                state(phase, it, b, 0, 0)
                spread(b, 0, "h3")
                state(phase, it, b, 0, 1)
                if more:
                    squares(phase, it, last, 1)
                spread(b, 0, "p1")
                spread(b, 0, "h4")
                state(phase, it, b, 0, 2)
                sums(phase, it, b, 1)
                if more:
                    mix(phase, it, last, 1, 0)
                project(b, 1, 1)
                if more:
                    mix(phase, it, last, 1, 1)
                outputs(phase, it, b, 0, 0)
                spread(b, 0, "h5")
                spread(b, 0, "p2")
                s_transposed(phase, it, b, 1)
                outputs(phase, it, b, 0, 1)
                project(b, 1, 2)
                spread(b, 0, "h6")
                spread(b, 0, "h7")
                if more:
                    norm2_transposed(phase, it, last, 0)
                    norm2_transposed(phase, it, last, 1)
                spread(b, 0, "p3")
                project(b, 1, 3)
                outputs(phase, it, b, 0, 2)
                if more:
                    feed(phase, it, 0)
                    feed(phase, it, 1)
                project(b, 1, 4)
                if more:
                    norm2_transposed(phase, it, last, 2)
                    norm2_transposed(phase, it, last, 3)
                outputs(phase, it, b, 0, 3)
                project(b, 1, 5)
                if more:
                    feed(phase, it, 2)
                    feed(phase, it, 3)
                project(b, 1, 6)
                released(phase, it, "1ST")

            pe.wait_ge(c_loaded, 16 * 4)
            norm_transposed("start", 0, 0)
            wait_xnt("start", 0)
            pe.wait_ge(wdt_lo_ready, 1)
            dt_project("start", 0)
            pe.wait_ge(w_lo_ready[0], KD)
            project(0, 0, 0)
            dt_transposed("start", 0)
            for t in range(1, NCONV + 1):
                project(0, 0, t)
            sums("start", 0, 0, 0)
            project(0, 0, NCONV + 1)
            pe.wait_ge(f_loaded, 16 * 14)
            fold_weights(range(KI))
            s_transposed("start", 0, 0, 0)
            fold_weights(range(KI, 2 * KI + 1))
            pe.wait_ge(w_lo_ready[1], KD)
            forward_scan("start", 0, 0, None)

            with pe.Fori(0, NB - 1) as it:
                reversed_scan("loop", it, it, it + 1)
                forward_scan("loop", it, it + 1, it)

            b = NB - 1
            reversed_scan("last", 0, b, None)
            squares("last", 0, b, 1)
            mix("last", 0, b, 1, 0)
            mix("last", 0, b, 1, 1)
            for c0 in (0, 2):
                for c in (c0, c0 + 1):
                    norm2_transposed("last", 0, b, c)
                for c in (c0, c0 + 1):
                    feed("last", 0, c)

        @block.scalar
        def _(act):
            def misc(phase, it, name):
                bank, used = misc_use(phase, it, name)
                act.wait_ge(mi_full[bank], used + 1)
                return mi[bank], mi_free[bank]

            def split_high(d):
                act.wait_ge(w_loaded[d], 16 * KD)
                for k in range(KD):
                    nc.scalar.activation(w_hi[:, d, k, :], raw_w[d][k], ACT.Copy).then_inc(w_hi_ready[d], 1)

            def split_dt_high():
                act.wait_ge(c_loaded, 16 * 4)
                act.wait_ge(setup_done, 1)
                nc.scalar.activation(wdt_hi[:], wdt, ACT.Copy).then_inc(wdt_hi_ready, 1)
                act.wait_ge(v_loaded, 16 * 8)
                nc.scalar.activation(arow[:], arow[:], ACT.Exp).then_inc(a_exp, 1)

            def fold_weights(uses):
                for n in uses:
                    d, t = divmod(n, KI)
                    ps, free = misc("start", 0, f"w{n}")
                    nc.scalar.activation(wc[:, d, t, :], ps[:, 0:D], ACT.Copy, scale=nw[:, d, t:t + 1]).then_inc(free, 1)

            def norm_high(phase, it):
                for k in range(KD):
                    ps, _ = misc(phase, it, f"a{k}")
                    nc.scalar.activation(xnt_hi[:, k, :], ps[:], ACT.Copy).then_inc(xnt_hi_ready, 1)

            def dt_bias(phase, it):
                if phase == "loop":
                    act.wait_ge(out_stored, 16 * NC * it + 1)
                ps, free = misc(phase, it, "dtm")
                nc.scalar.activation(dt_t, ps[0:2 * NH, :], ACT.Identity, bias=dtb_sb[:, 0:1]).then_inc(free, 1)

            def soft_exp(b):
                act.wait_ge(na_ready, b + 1)
                nc.scalar.activation(e[:], na[:], ACT.Exp).then_inc(e_ready, 1)

            def soft_log(b):
                act.wait_ge(u_ready, b + 1)
                nc.scalar.activation(lnu[:], u1[:], ACT.Ln).then_inc(ln_ready, 1)

            def s_pieces(phase, it, d):
                ps, free = misc(phase, it, f"{d}ST")
                nc.scalar.activation(st_bf[:, d, :], ps[:, 0:T // 2].bitcast(BF16), ACT.Copy).then_inc(free, 1)

            def conv_start(b, d, t):
                bank, used = pj_use(b, d, t)
                u = 2 * b + d
                if t == 0 and not (isinstance(b, int) and b == d == 0):
                    act.wait_ge(xs_ready, KI * u)
                act.wait_ge(pj_full[bank], used + 1)
                nc.scalar.activation(xc[:, t, :], pj[bank][:], ACT.Identity, bias=cb[:, d, t:t + 1],
                                     scale=cw[:, d, t, KW - 1:KW]).then_inc(conv_first, 1)

            def conv_end(b, d, t):
                bank, used = pj_use(b, d, t)
                if t == 0 and not (isinstance(b, int) and b == 0):
                    act.wait_ge(yg_ready, KI * (2 * b + d - 1))
                act.wait_ge(pj_free[bank], used + 2)
                dst, ready = (bcm[:, d, :], bc_ready) if t == 0 else (xs[:, d, t - 1, :], xs_ready)
                nc.scalar.activation(dst, xc[:, t, :], ACT.Silu).then_inc(ready, 1)

            def gate(b, d, t):
                bank, used = pj_use(b, d, t)
                act.wait_ge(pj_full[bank], used + 1)
                nc.scalar.activation(sz[:, d, t - NCONV, :], pj[bank][:], ACT.Silu).then_inc(pj_free[bank], 1)

            def decays(b, d):
                act.wait_ge(wd_ready, 2 * b + d + 1)
                nc.scalar.activation(w_end[:, d], wd[:, d], ACT.Exp)
                nc.scalar.activation(e_end[:, d], s_all[:, d, 1].rearrange("p c h -> p (c h)"), ACT.Exp).then_inc(w_ready, 1)

            def spread(b, d, name):
                u = 2 * b + d
                bank, used = sb_use(b, d, name)
                n = int(name[1])
                act.wait_ge(sb_full[bank], used + 1)
                if name[0] == "h":
                    act.wait_ge(m_ready, NH * u + n + 1)
                    for c in range(NC):
                        o = c * NH + n
                        i = nc.scalar.activation(lx[:, n % 2, Q * c:Q * c + Q], sbk[bank][:, Q * c:Q * c + Q], ACT.Exp,
                                                 bias=neg_s[:, d, o:o + 1])
                    i.then_inc(sb_free[bank], 1)
                else:
                    act.wait_ge(c2_ready, KI * u + n + 1)
                    nc.scalar.activation(es[:, n % 2, :], sbk[bank][:], ACT.Exp).then_inc(sb_free[bank], 1)

            def b_tokens(phase, it, d):
                ps, free = misc(phase, it, f"{d}bt")
                src = ps[:].rearrange("p (c n) -> p c n", c=NC)[:, :, 0:NS]
                nc.scalar.activation(btok[:], src, ACT.Copy).then_inc(free, 1)

            def norm2(phase, it, c):
                ps, free = misc(phase, it, f"t{c}")
                nc.scalar.activation(xn2t[:, c % 2], ps[:, 0:D].rearrange("p (k n) -> p k n", k=KD), ACT.Copy).then_inc(free, 1)

            def spreads(b, d, *names):
                for name in names:
                    spread(b, d, name)

            def conv_ends(b, d, *tiles):
                for t in tiles:
                    conv_end(b, d, t)

            def gates(b, d, *tiles):
                for t in tiles:
                    gate(b, d, t)

            def scan_start(phase, it, b, d):
                b_tokens(phase, it, d)
                gates(b, d, NT - 2, NT - 1)
                decays(b, d)
                spreads(b, d, "h0", "h1", "p0")

            def reversed_scan(phase, it, b, nxt):
                more = phase == "loop"
                scan_start(phase, it, b, 1)
                spreads(b, 1, "h2", "h3", "p1")
                if more:
                    norm_high(phase, it)
                spreads(b, 1, "h4")
                if more:
                    dt_bias(phase, it)
                    conv_start(nxt, 0, 0)
                spreads(b, 1, "h5", "p2")
                if more:
                    conv_start(nxt, 0, 1)
                spreads(b, 1, "h6")
                if more:
                    soft_exp(nxt)
                spreads(b, 1, "h7")
                if more:
                    conv_start(nxt, 0, 2)
                spreads(b, 1, "p3")
                if more:
                    soft_log(nxt)
                    conv_start(nxt, 0, 3)
                    conv_ends(nxt, 0, 0, 1, 2)
                    conv_start(nxt, 0, 4)
                    conv_ends(nxt, 0, 3, 4)
                    gates(nxt, 0, 5, 6)
                    s_pieces(phase, it, 0)

            def forward_scan(phase, it, b):
                more = phase == "loop"
                scan_start(phase, it, b, 0)
                conv_start(b, 1, 0)
                spreads(b, 0, "h2", "h3", "p1", "h4")
                conv_start(b, 1, 1)
                spreads(b, 0, "h5", "p2")
                s_pieces(phase, it, 1)
                conv_start(b, 1, 2)
                spreads(b, 0, "h6", "h7")
                if more:
                    norm2(phase, it, 0)
                    norm2(phase, it, 1)
                spreads(b, 0, "p3")
                conv_start(b, 1, 3)
                conv_ends(b, 1, 0, 1, 2)
                conv_start(b, 1, 4)
                conv_ends(b, 1, 3, 4)
                if more:
                    norm2(phase, it, 2)
                    norm2(phase, it, 3)
                gates(b, 1, 5, 6)

            split_high(0)
            split_dt_high()
            norm_high("start", 0)
            dt_bias("start", 0)
            conv_start(0, 0, 0)
            soft_exp(0)
            conv_start(0, 0, 1)
            conv_start(0, 0, 2)
            soft_log(0)
            conv_start(0, 0, 3)
            split_high(1)
            conv_ends(0, 0, 0, 1, 2)
            conv_start(0, 0, 4)
            conv_ends(0, 0, 3, 4)
            gates(0, 0, 5, 6)
            fold_weights(range(KI))
            s_pieces("start", 0, 0)
            fold_weights(range(KI, 2 * KI))
            forward_scan("start", 0, 0)

            with act.Fori(0, NB - 1) as it:
                reversed_scan("loop", it, it, it + 1)
                forward_scan("loop", it, it + 1)

            reversed_scan("last", 0, NB - 1, None)
            for c in range(NC):
                norm2("last", 0, c)

        @block.vector
        def _(dve):
            for s in (*pj_free, *sb_free, *py_free, *mi_free):
                dve.sem_inc(s, 1)
            for s in (m_ready, c2_ready):
                dve.sem_inc(s, 2)
            dve.sem_inc(out_stored, 1)

            def misc(phase, it, name):
                bank, used = misc_use(phase, it, name)
                dve.wait_ge(mi_full[bank], used + 1)
                return mi[bank], mi_free[bank]

            def setup():
                dve.memset(wdt[:, :, 2 * NH:P], 0.0)
                dve.memset(halves[:], -0.5).then_inc(setup_done, 1)

            def zeros():
                dve.memset(spc[:], 0.0)
                dve.memset(cz[NS:P, :], 0.0)
                dve.memset(hst[:], 0.0).then_inc(setup_done, 1)

            def selectors():
                dve.wait_ge(c_loaded, 16 * 4)
                dve.tensor_copy(identb[:], ident)
                for d in range(2):
                    dve.tensor_scalar(hide[:, d, :], tri[d], -FAR, FAR, ALU.mult, ALU.add)
                dve.tensor_copy(sel[:], selc[:].unsqueeze(2).broadcast_to([P, NH, P]))
                dve.tensor_copy(selp[:], selc[:].unsqueeze(2).broadcast_to([P, NH, HP])).then_inc(sel_done, 1)

            def split_low(d):
                for k in range(KD):
                    dve.wait_ge(w_hi_ready[d], k + 1)
                    dve.tensor_tensor(w_lo[:, d, k, :], raw_w[d][k], w_hi[:, d, k, :].bitcast(F32),
                                      ALU.subtract).then_inc(w_lo_ready[d], 1)

            def split_dt_low():
                dve.wait_ge(wdt_hi_ready, 1)
                dve.tensor_tensor(wdt_lo[:], wdt, wdt_hi[:].bitcast(F32), ALU.subtract).then_inc(wdt_lo_ready, 1)
                dve.wait_ge(a_exp, 1)
                dve.tensor_scalar(abc[:], arow[:].unsqueeze(1).broadcast_to([P, NC, 2 * NH]), -1.0, None,
                                  ALU.mult).then_inc(a_done, 1)

            def fold_ffn():
                ps, free = misc("start", 0, f"w{2 * KI}")
                dve.tensor_tensor(wff[:], ps[:].rearrange("p (k n) -> p k n", k=KD), raw_ffT, ALU.add).then_inc(free, 1)

            def norm_stats(src, st, mv, stats, aggr, b):
                for c in range(NC):
                    dve.bn_stats(st[:, c, :], src[:, c, :]).then_inc(stats, 1)
                for c in range(NC):
                    dve.wait_ge(stats, NC * b + c + 1)
                    alone(dve)
                    dve.bn_aggr(mv[:, c, :], st[:, c, :]).then_inc(aggr, 1)

            def norm_scale(dst, src, mv, rstd, ready):
                for c in range(NC):
                    dve.tensor_scalar(dst[:, c, :], src[:, c, :], mv[:, c, 0:1], rstd[:, c:c + 1],
                                      ALU.subtract, ALU.mult).then_inc(ready, 1)

            def norm1_stats(b):
                dve.wait_ge(x_loaded, 16 * (b + 1))
                norm_stats(xin, st1, mv1, ln1_stats, ln1_mv, b)

            def norm1_scale(b):
                dve.wait_ge(ln1_rstd, b + 1)
                norm_scale(xn, xin, mv1, rstd1, xn_ready)

            def norm_low(phase, it, b):
                for k in range(KD):
                    ps, free = misc(phase, it, f"a{k}")
                    dve.wait_ge(xnt_hi_ready, KD * b + k + 1)
                    dve.tensor_tensor(xnt_lo[:, k, :], ps[:], xnt_hi[:, k, :].bitcast(F32), ALU.subtract).then_inc(free, 1)

            def soft_in(phase, it, b):
                ps, free = misc(phase, it, "dtt")
                dve.tensor_copy(v[:].rearrange("p c n -> p (c n)"), ps[:, 0:2 * NCH]).then_inc(free, 1)
                bank, used = misc_use(phase, it, "dtt")
                dve.wait_ge(free, used + 2)
                dve.scalar_tensor_tensor(na[:], v[:], -1.0, v[:], ALU.mult, ALU.min).then_inc(na_ready, 1)

            def soft_mid(b):
                dve.wait_ge(e_ready, b + 1)
                dve.tensor_scalar(u1[:], e[:], 1.0, None, ALU.add).then_inc(u_ready, 1)
                dve.wait_ge(u_ready, b + 1)
                dve.tensor_scalar(du[:], u1[:], -1.0, None, ALU.add).then_inc(dt_step, 1)
                dve.wait_ge(dt_step, 5 * b + 1)
                dve.scalar_tensor_tensor(dd[:], du[:], 0.0, du[:], ALU.is_equal, ALU.add).then_inc(dt_step, 1)
                dve.wait_ge(dt_step, 5 * b + 2)
                dve.reciprocal(rq[:], dd[:]).then_inc(dt_step, 1)

            def soft_out(b):
                dve.wait_ge(ln_ready, b + 1)
                dve.wait_ge(dt_step, 5 * b + 3)
                dve.tensor_tensor(r1[:], lnu[:], rq[:], ALU.mult).then_inc(dt_step, 1)
                dve.wait_ge(dt_step, 5 * b + 4)
                dve.scalar_tensor_tensor(r2[:], du[:], 0.0, r1[:], ALU.is_equal, ALU.add).then_inc(dt_step, 1)
                dve.wait_ge(dt_step, 5 * b + 5)
                dve.tensor_tensor(r3[:], r2[:], e[:], ALU.mult).then_inc(r_ready, 1)

            def dt_values(b, d):
                u = 2 * b + d
                cols = slice(NH * d, NH * d + NH)
                dve.wait_ge(r_ready, b + 1)
                dve.scalar_tensor_tensor(dt[:, d], v[:, :, cols], 0.0, r3[:, :, cols], ALU.max, ALU.add).then_inc(fin_step, 1)
                dve.wait_ge(fin_step, 2 * u + 1)
                dve.tensor_tensor(adt[:, d], dt[:, d], abc[:, :, cols], ALU.mult).then_inc(fin_step, 1)
                dve.wait_ge(fin_step, 2 * u + 2)
                dve.tensor_scalar(al[:, d], adt[:, d], A_FLOOR, None, ALU.max).then_inc(al_ready, 1)

            def s_values(phase, it, b, d):
                ps, free = misc(phase, it, f"{d}S")
                _, used = misc_use(phase, it, f"{d}S")
                dve.tensor_copy(s_all[:, d].rearrange("p s c h -> p (s c h)"), ps[:, 0:2 * NCH]).then_inc(free, 1)
                dve.wait_ge(free, used + 2)
                s, end = (s_all[:, d, i].rearrange("p c h -> p (c h)") for i in range(2))
                dve.tensor_scalar(neg_s[:, d], s, -1.0, None, ALU.mult).then_inc(s_ready, 1)
                dve.tensor_tensor(wd[:, d], end, s, ALU.subtract).then_inc(wd_ready, 1)

            def conv(b, d, t):
                u = 2 * b + d
                bank, used = pj_use(b, d, t)
                dve.wait_ge(conv_first, NCONV * u + t + 1)
                for s in range(1, KW):
                    to = slice(s, T) if d == 0 else slice(0, T - s)
                    of = slice(0, T - s) if d == 0 else slice(s, T)
                    if s > 1:
                        dve.wait_ge(conv_step, (KW - 2) * (NCONV * u + t) + s - 1)
                    i = dve.scalar_tensor_tensor(xc[:, t, to], pj[bank][:, of], cw[:, d, t, KW - 1 - s:KW - s],
                                                 xc[:, t, to], ALU.mult, ALU.add)
                    i.then_inc(pj_free[bank] if s == KW - 1 else conv_step, 1)

            def x_tokens(phase, it, d, j):
                ps, free = misc(phase, it, f"{d}x{j}")
                c = ORDER[d][j]
                dve.tensor_tensor(xdt[:, c, :].rearrange("p (h q) -> p h q", h=NH), ps[:].rearrange("p (h q) -> p h q", h=NH),
                                  dt[:, d, c, :].unsqueeze(2).broadcast_to([P, NH, HP]), ALU.mult).then_inc(free, 1)

            def scores(phase, it, b, d):
                ps, free = misc(phase, it, f"{d}g")
                dve.tensor_copy(gm[:], ps[:]).then_inc(free, 1)

            def weights(phase, it, b, d, h):
                u = 2 * b + d
                if h == 0:
                    bank, used = misc_use(phase, it, f"{d}g")
                    dve.wait_ge(mi_free[bank], used + 2)
                bank, used = sb_use(b, d, f"h{h}")
                dve.wait_ge(sb_free[bank], used + 2)
                dve.tensor_tensor(mx[:, h % 4, :], lx[:, h % 2, :], gm[:], ALU.mult).then_inc(m_ready, 1)

            def state(phase, it, b, d, j):
                u = 2 * b + d
                ps, free = misc(phase, it, f"{d}s{j}")
                if j:
                    dve.wait_ge(hs_ready, (NC - 2) * u + j)
                view = ps[:, 0:DI // 2].rearrange("p (r q) -> p r q", q=HP)
                for half in range(2):
                    lanes, cols = slice(HP * half, HP * half + HP), slice(HP * half, HP * half + HP)
                    if j == 0:
                        i = dve.tensor_copy(hst[lanes, j, :, cols], view[lanes])
                    else:
                        i = dve.tensor_tensor(hst[lanes, j, :, cols], view[lanes], hs[lanes, :, cols], ALU.add)
                i.then_inc(free, 1)

            def outputs(b, d, p):
                u = 2 * b + d
                bank, used = py_use(b, d, p)
                dve.wait_ge(py_full[bank], used + 1)
                dve.scalar_tensor_tensor(yg[:, d, p, :], xs[:, d, p, :], dsk[:, d, p:p + 1], py[bank][:], ALU.mult,
                                         ALU.add).then_inc(py_free[bank], 1)
                dve.wait_ge(py_free[bank], used + 2)
                dve.tensor_tensor(yg[:, d, p, :], yg[:, d, p, :], sz[:, d, p, :], ALU.mult).then_inc(yg_ready, 1)

            def squares(phase, it, d):
                ps, free = misc(phase, it, f"{d}ss")
                dve.tensor_copy(ss[:, d, :], ps[:, 0:NC]).then_inc(free, 1)

            def mix(phase, it, b, d, half):
                ps, free = misc(phase, it, f"{d}o{half}")
                if half == 0:
                    dve.wait_ge(xres_ready, b + 1)
                    dve.wait_ge(rms_ready, 2 * b + d + 1)
                for i in range(2):
                    c = 2 * half + i
                    mm = dve.scalar_tensor_tensor(xres[:, c, :], ps[:, D * i:D * i + D], rms[:, d, c:c + 1], xres[:, c, :],
                                                  ALU.mult, ALU.add)
                mm.then_inc(free, 1)

            def norm2_stats(phase, it, b):
                for half in range(2):
                    bank, used = misc_use(phase, it, f"1o{half}")
                    dve.wait_ge(mi_free[bank], used + 2)
                norm_stats(xres, st2, mv2, ln2_stats, ln2_mv, b)

            def norm2_scale(b):
                dve.wait_ge(ln2_rstd, b + 1)
                norm_scale(xn2, xres, mv2, rstd2, xn2_ready)

            def feed(phase, it, b, c):
                ps, free = misc(phase, it, f"f{c}")
                if c == 0:
                    dve.wait_ge(otb_ready, b + 1)
                dve.tensor_tensor(ot[:, c, :], ps[:, 0:D], ot[:, c, :], ALU.add).then_inc(free, 1)

            def scan_start(phase, it, b, d):
                for j in range(NC):
                    x_tokens(phase, it, d, j)
                scores(phase, it, b, d)
                weights(phase, it, b, d, 0)
                weights(phase, it, b, d, 1)

            def reversed_scan(phase, it, b, nxt):
                more = phase == "loop"
                if more:
                    norm1_stats(nxt)
                scan_start(phase, it, b, 1)
                if more:
                    norm1_scale(nxt)
                state(phase, it, b, 1, 0)
                weights(phase, it, b, 1, 2)
                state(phase, it, b, 1, 1)
                squares(phase, it, 0)
                if more:
                    norm_low(phase, it, nxt)
                weights(phase, it, b, 1, 3)
                state(phase, it, b, 1, 2)
                mix(phase, it, b, 0, 0)
                if more:
                    conv(nxt, 0, 0)
                outputs(b, 1, 0)
                mix(phase, it, b, 0, 1)
                weights(phase, it, b, 1, 4)
                weights(phase, it, b, 1, 5)
                if more:
                    soft_in(phase, it, nxt)
                    conv(nxt, 0, 1)
                outputs(b, 1, 1)
                weights(phase, it, b, 1, 6)
                weights(phase, it, b, 1, 7)
                if more:
                    soft_mid(nxt)
                    conv(nxt, 0, 2)
                outputs(b, 1, 2)
                if more:
                    conv(nxt, 0, 3)
                    soft_out(nxt)
                    dt_values(nxt, 0)
                    conv(nxt, 0, 4)
                outputs(b, 1, 3)
                if more:
                    s_values(phase, it, nxt, 0)

            def forward_scan(phase, it, b, last):
                more = phase == "loop"
                dt_values(b, 1)
                scan_start(phase, it, b, 0)
                state(phase, it, b, 0, 0)
                weights(phase, it, b, 0, 2)
                state(phase, it, b, 0, 1)
                if more:
                    squares(phase, it, 1)
                conv(b, 1, 0)
                weights(phase, it, b, 0, 3)
                state(phase, it, b, 0, 2)
                s_values(phase, it, b, 1)
                if more:
                    mix(phase, it, last, 1, 0)
                conv(b, 1, 1)
                if more:
                    mix(phase, it, last, 1, 1)
                outputs(b, 0, 0)
                if more:
                    norm2_stats(phase, it, last)
                weights(phase, it, b, 0, 4)
                weights(phase, it, b, 0, 5)
                outputs(b, 0, 1)
                conv(b, 1, 2)
                if more:
                    norm2_scale(last)
                weights(phase, it, b, 0, 6)
                weights(phase, it, b, 0, 7)
                conv(b, 1, 3)
                outputs(b, 0, 2)
                if more:
                    feed(phase, it, last, 0)
                    feed(phase, it, last, 1)
                conv(b, 1, 4)
                outputs(b, 0, 3)
                if more:
                    feed(phase, it, last, 2)
                    feed(phase, it, last, 3)

            setup()
            norm1_stats(0)
            selectors()
            norm1_scale(0)
            split_low(0)
            split_dt_low()
            norm_low("start", 0, 0)
            zeros()
            conv(0, 0, 0)
            soft_in("start", 0, 0)
            conv(0, 0, 1)
            soft_mid(0)
            conv(0, 0, 2)
            conv(0, 0, 3)
            soft_out(0)
            dt_values(0, 0)
            conv(0, 0, 4)
            s_values("start", 0, 0, 0)
            split_low(1)
            fold_ffn()
            forward_scan("start", 0, 0, None)

            with dve.Fori(0, NB - 1) as it:
                reversed_scan("loop", it, it, it + 1)
                forward_scan("loop", it, it + 1, it)

            b = NB - 1
            reversed_scan("last", 0, b, None)
            squares("last", 0, 1)
            mix("last", 0, b, 1, 0)
            mix("last", 0, b, 1, 1)
            norm2_stats("last", 0, b)
            norm2_scale(b)
            for c in range(NC):
                feed("last", 0, b, c)

        @block.gpsimd
        def _(pool):
            def keep_x(b):
                pool.wait_ge(x_loaded, 16 * (b + 1))
                pool.tensor_tensor(xres[:], xin[:], bo_sb[:].unsqueeze(1).broadcast_to([P, NC, D]), ALU.add).then_inc(xres_ready, 1)

            def inv_sqrt(src, mid, dst, scale, mid_ready, ready, b):
                alone(pool)
                pool.tensor_scalar(mid, src, scale, EPS, ALU.mult, ALU.add).then_inc(mid_ready, 1)
                pool.wait_ge(mid_ready, b + 1)
                n = mid.shape[-1]
                pool.tensor_tensor(dst, mid, halves[:, 0:n], ALU.pow).then_inc(ready, 1)

            def norm1(b):
                pool.wait_ge(ln1_mv, NC * (b + 1))
                inv_sqrt(mv1[:, :, 1], ve1[:], rstd1[:], 1.0, ln1_ve, ln1_rstd, b)

            def norm2(b):
                pool.wait_ge(ln2_mv, NC * (b + 1))
                inv_sqrt(mv2[:, :, 1], ve2[:], rstd2[:], 1.0, ln2_ve, ln2_rstd, b)

            def root_mean_square(phase, it, b, d):
                bank, used = misc_use(phase, it, f"{d}ss")
                pool.wait_ge(mi_free[bank], used + 2)
                inv_sqrt(ss[:, d, :], ms[:, d, :], rms[:, d, :], 1.0 / DI, ms_ready, rms_ready, 2 * b + d)

            def pieces(b, d):
                u = 2 * b + d
                steps = 2 * PIECES - 2
                pool.wait_ge(s_ready, u + 1)
                left = s_all[:, d, 0]
                n = 0
                for q, rest in enumerate((rem1, rem2, None)):
                    piece = spc[:, :, NH * q:NH * q + NH]
                    alone(pool)
                    pool.tensor_copy(piece, left).then_inc(spc_step if rest is not None else spc_ready, 1)
                    if rest is not None:
                        pool.wait_ge(spc_step, steps * u + n + 1)
                        pool.tensor_tensor(rest[:], left, piece, ALU.subtract).then_inc(spc_step, 1)
                        n += 2
                        pool.wait_ge(spc_step, steps * u + n)
                        left = rest[:]

            def decayed_x(phase, it, b, d, j):
                if j == 0:
                    pool.wait_ge(w_ready, 2 * b + d + 1)
                bank, used = misc_use(phase, it, f"{d}x{j}")
                pool.wait_ge(mi_free[bank], used + 2)
                c = ORDER[d][j]
                o = c * NH
                hq = "p (h q) -> p h q"
                pool.tensor_tensor(xw[:, j, :].rearrange(hq, h=NH), xdt[:, c, :].rearrange(hq, h=NH),
                                   w_end[:, d, o:o + NH].unsqueeze(2).broadcast_to([P, NH, HP]), ALU.mult).then_inc(xw_ready, 1)

            def decayed_c(b, d, p):
                bank, used = sb_use(b, d, f"p{p}")
                pool.wait_ge(sb_free[bank], used + 2)
                if p >= 2:
                    bank, used = py_use(b, d, p - 2)
                    pool.wait_ge(py_full[bank], used + 1)
                pool.tensor_tensor(c2[:, p % 2, :], cc[:, d, :], es[:, p % 2, :], ALU.mult).then_inc(c2_ready, 1)

            def decayed_state(phase, it, b, d, j):
                bank, used = misc_use(phase, it, f"{d}s{j - 1}")
                pool.wait_ge(mi_free[bank], used + 2)
                o = ORDER[d][j] * NH
                pool.tensor_tensor(hs[:].rearrange("p r (e q) -> p (r e) q", e=2),
                                   hst[:, j - 1].rearrange("p r (e q) -> p (r e) q", e=2),
                                   e_end[:, d, o:o + NH].unsqueeze(2).broadcast_to([P, NH, HP]), ALU.mult).then_inc(hs_ready, 1)

            def squares(b, d, tiles):
                u = 2 * b + d
                n = 2 * KI - 2
                for t in tiles:
                    pool.wait_ge(yg_ready, KI * u + t + 1)
                    if t >= 2:
                        pool.wait_ge(sq_step, n * u + 2 * t - 1)
                    to = sqsum if t == 0 else sq
                    pool.tensor_tensor(to[:], yg[:, d, t, :], yg[:, d, t, :], ALU.mult).then_inc(sq_step, 1)
                    if t:
                        pool.wait_ge(sq_step, n * u + 2 * t)
                        i = pool.tensor_tensor(sqsum[:], sqsum[:], sq[:], ALU.add)
                        i.then_inc(sqsum_ready if t == KI - 1 else sq_step, 1)

            def result_bias(phase, it, b):
                bank, used = misc_use(phase, it, "1o1")
                pool.wait_ge(mi_free[bank], used + 2)
                pool.wait_ge(out_stored, 16 * NC * b + 1)
                pool.tensor_tensor(ot[:], xres[:], ffb_sb[:].unsqueeze(1).broadcast_to([P, NC, D]), ALU.add).then_inc(otb_ready, 1)

            def scan_start(phase, it, b, d):
                for j in range(NC - 1):
                    decayed_x(phase, it, b, d, j)
                decayed_state(phase, it, b, d, 1)
                decayed_c(b, d, 0)
                decayed_state(phase, it, b, d, 2)

            def reversed_scan(phase, it, b, nxt):
                more = phase == "loop"
                if more:
                    norm1(nxt)
                scan_start(phase, it, b, 1)
                root_mean_square(phase, it, b, 0)
                decayed_c(b, 1, 1)
                decayed_c(b, 1, 2)
                decayed_c(b, 1, 3)
                squares(b, 1, range(KI - 1))
                if more:
                    pieces(nxt, 0)
                squares(b, 1, [KI - 1])

            def forward_scan(phase, it, b, last):
                more = phase == "loop"
                scan_start(phase, it, b, 0)
                if more:
                    root_mean_square(phase, it, last, 1)
                decayed_c(b, 0, 1)
                pieces(b, 1)
                if more:
                    norm2(last)
                decayed_c(b, 0, 2)
                if more:
                    result_bias(phase, it, last)
                decayed_c(b, 0, 3)
                if more:
                    pool.wait_ge(xn2_ready, NC * (last + 1))
                    pool.wait_ge(otb_ready, last + 1)
                    keep_x(b)
                squares(b, 0, range(KI))

            pool.wait_ge(setup_done, 1)
            norm1(0)
            pool.wait_ge(setup_done, 2)
            pieces(0, 0)
            pool.wait_ge(f_loaded, 16 * 14)
            keep_x(0)
            forward_scan("start", 0, 0, None)

            with pool.Fori(0, NB - 1) as it:
                reversed_scan("loop", it, it, it + 1)
                forward_scan("loop", it, it + 1, it)

            b = NB - 1
            reversed_scan("last", 0, b, None)
            root_mean_square("last", 0, b, 1)
            norm2(b)
            result_bias("last", 0, b)


_DIRS = ("f", "b")
_OUT = ((NB, T, D), "float32")


def _arrays(inputs):
    import numpy as np

    def get(name):
        return np.ascontiguousarray(inputs["L0_" + name])

    tok = np.arange(P)
    consts = np.zeros((P, 4, P), np.float32)
    consts[:, 0] = np.eye(P)
    consts[:, 1] = tok[:, None] <= tok[None, :]
    consts[:, 2] = tok[:, None] >= tok[None, :]
    consts[:, 3] = 1.0
    selcol = np.zeros((P, NH), np.float32)
    for q in range(PIECES):
        for h in range(NH):
            selcol[NH * q + h, h] = 1.0

    tiles = [KI] + list(range(KI))
    arrays = {"x": get("attn_x"), "consts": consts, "selcol": selcol}
    for s in _DIRS:
        arrays[s + "win"] = get(f"attn_{s}Win")
        arrays[s + "convw"] = get(f"attn_{s}convw").reshape(KW, NCONV, P).transpose(2, 1, 0)[:, tiles]
        arrays[s + "convb"] = get(f"attn_{s}convb").reshape(NCONV, P).transpose(1, 0)[:, tiles]
        arrays[s + "dtb"] = get(f"attn_{s}dtb")
        arrays[s + "alog"] = get(f"attn_{s}Alog")
        arrays[s + "dskip"] = get(f"attn_{s}D").reshape(KI, 2).transpose(1, 0)
        arrays[s + "normw"] = get(f"attn_{s}normw").reshape(KI, P).transpose(1, 0)
        arrays[s + "woutT"] = get(f"attn_{s}Wout").transpose(1, 0)
    arrays |= {"wo": get("attn_Wo"), "bo": get("attn_bo"), "ffT": get("ffn_W").transpose(1, 0), "ffb": get("ffn_b"),
               "vrT": get("ffn_V_r").transpose(1, 0), "cT": get("ffn_C").transpose(1, 0)}
    return {k: np.ascontiguousarray(v) for k, v in arrays.items()}


def kernel(**inputs):
    import numpy as np
    import concourse.bacc as bacc
    from concourse.bass_utils import run_bass_kernel_spmd

    nc = bacc.Bacc("TRN2", target_bir_lowering=False, num_devices=1)
    arrays = {f"in_{k}": v for k, v in _arrays(inputs).items()}
    ap = {k[3:]: nc.dram_tensor(k, v.shape, mybir.dt.from_np(v.dtype), kind="ExternalInput").ap() for k, v in arrays.items()}
    out = nc.dram_tensor("out", _OUT[0], mybir.dt.from_np(np.dtype(_OUT[1])), kind="ExternalOutput").ap()

    def both(name):
        return [ap[s + name] for s in _DIRS]

    build(nc, ap["x"], ap["consts"], ap["selcol"], both("win"), both("convw"), both("convb"), both("dtb"), both("alog"),
          both("dskip"), both("normw"), both("woutT"), ap["wo"], ap["bo"], ap["ffT"], ap["ffb"], ap["vrT"], ap["cT"], out)
    result = run_bass_kernel_spmd(nc, [arrays], core_ids=[0])
    return result.results[0]["out"]
```

```python
from contextlib import ExitStack

import concourse.bass as bass
from concourse import mybir

F32 = mybir.dt.float32
F32R = mybir.dt.float32r
BF16 = mybir.dt.bfloat16
ALU = mybir.AluOpType
ACT = mybir.ActivationFunctionType

P = 128
NB, T, D = 8, 512, 256
DI, NS, NH, HP = 512, 64, 8, 64
KW = 4
DPROJ = 2 * DI + 2 * NS + NH
Q = 128
NC = T // Q
KD = D // P
KI = DI // P
RANK = 32
EPS = 1e-5
A_FLOOR = -105.0
FAR = -32768.0
PIECES = 3

COLS = [2 * DI] + [DI + P * t for t in range(KI)] + [P * t for t in range(KI)]
NCONV = 1 + KI
NT = len(COLS)

ORDER = [list(range(NC)), list(reversed(range(NC)))]
LATER = [slice(Q, T), slice(0, T - Q)]
BC = ["h0", "h1", "p0", "h2", "h3", "p1", "h4", "h5", "p2", "h6", "h7", "p3"]

WEIGHTS = [f"w{n}" for n in range(2 * KI + 1)]
FFN = ["t0", "t1", "f0", "f1", "t2", "t3", "f2", "f3"]
START = (["a0", "a1", "dtm", "dtt"] + WEIGHTS[0:2 * KI] + ["0S"] + WEIGHTS[2 * KI:]
         + ["0bt", "0x0", "0x1", "0ST", "0x2", "0x3", "0g", "0s0", "0s1", "0s2", "1S", "1ST"])
LOOP = (["1bt", "1x0", "1x1", "1x2", "1x3", "1g", "a0", "a1", "1s0", "1s1", "dtm", "0ss", "1s2", "0o0", "dtt", "0o1", "0S"]
        + ["0bt", "0x0", "0x1", "0ST", "0x2", "0x3", "0g", "0s0", "0s1", "1ss", "0s2", "1S", "1o0", "1o1", "1ST"] + FFN)
LAST = ["1bt", "1x0", "1x1", "1x2", "1x3", "1g", "1s0", "1s1", "0ss", "1s2", "0o0", "0o1", "1o0", "1o1"] + FFN
assert len(START) % 2 == 0 and len(LOOP) % 2 == 0


def misc_use(phase, it, name):
    if phase == "start":
        n = START.index(name)
        return n % 2, n // 2
    if phase == "loop":
        n = len(START) + LOOP.index(name)
        return n % 2, it * (len(LOOP) // 2) + n // 2
    n = len(START) + (NB - 1) * len(LOOP) + LAST.index(name)
    return n % 2, n // 2


def build(nc, x, consts, selcol, win, convw, convb, dtb, alog, dskip, normw, woutT, wo, bo, ffT, ffb, vrT, cT, out):
    with ExitStack() as ctx:
        def sb(name, shape, dt=F32):
            return ctx.enter_context(nc.sbuf_tensor(name, shape, dt))

        def sem(name):
            return ctx.enter_context(nc.semaphore(name))

        cst = sb("cst", [P, 4, P])
        ident, upto, since, ones = (cst[:, i, :] for i in range(4))
        tri = [upto, since]
        identb = sb("identb", [P, P], BF16)
        selc = sb("selc", [P, NH])
        sel = sb("sel", [P, NH, P], BF16)
        selp = sb("selp", [P, NH, HP], BF16)
        hide = sb("hide", [P, 2, Q], BF16)
        halves = sb("halves", [P, 16])
        w_hi = sb("w_hi", [P, 2, KD, DPROJ - NH], F32R)
        w_lo = sb("w_lo", [P, 2, KD, DPROJ - NH], F32R)
        wdt_hi = sb("wdt_hi", [P, KD, P], F32R)
        wdt_lo = sb("wdt_lo", [P, KD, P], F32R)
        cw = sb("cw", [P, 2, NCONV, KW])
        cb = sb("cb", [P, 2, NCONV])
        dtb_sb = sb("dtb_sb", [2 * NH, 1])
        arow = sb("arow", [P, 2 * NH])
        abc = sb("abc", [P, NC, 2 * NH])
        dsk = sb("dsk", [P, 2, KI])
        nw = sb("nw", [P, 2, KI])
        wc = sb("wc", [P, 2, KI, D])
        wff = sb("wff", [P, KD, D])
        bo_sb = sb("bo_sb", [P, D])
        ffb_sb = sb("ffb_sb", [P, D])

        xin = sb("xin", [P, NC, D])
        xres = sb("xres", [P, NC, D])
        st1 = sb("st1", [P, NC, 6])
        mv1 = sb("mv1", [P, NC, 2])
        ve1 = sb("ve1", [P, NC])
        rstd1 = sb("rstd1", [P, NC])
        xn = sb("xn", [P, NC, D])
        xnt_hi = sb("xnt_hi", [P, KD, T], F32R)
        xnt_lo = sb("xnt_lo", [P, KD, T], F32R)
        NCH = NC * NH
        v, na, e, u1, du, dd, rq, r2, r3 = (sb(n, [P, NC, 2 * NH]) for n in "v na e u1 du dd rq r2 r3".split())
        lnu, r1 = na, dd
        rem1 = sb("rem1", [P, NC, NH])
        rem2 = sb("rem2", [P, NC, NH])
        spc = sb("spc", [P, NC, P], BF16)
        ss = sb("ss", [P, 2, NC])
        ms = sb("ms", [P, 2, NC])
        rms = sb("rms", [P, 2, NC])
        st2 = sb("st2", [P, NC, 6])
        mv2 = sb("mv2", [P, NC, 2])
        ve2 = sb("ve2", [P, NC])
        rstd2 = sb("rstd2", [P, NC])
        xn2 = xn
        xn2t = sb("xn2t", [P, 2, KD, P])
        ot = sb("ot", [P, NC, D])
        dt_t = ot[0:2 * NH, 0:2, :].rearrange("p c n -> p (c n)")

        dt, adt, al = (sb(n, [P, 2, NC, NH]) for n in "dt adt al".split())
        s_all = sb("s_all", [P, 2, 2, NC, NH])
        neg_s = sb("neg_s", [P, 2, NCH])
        wd = sb("wd", [P, 2, NCH])
        w_end = sb("w_end", [P, 2, NCH])
        e_end = sb("e_end", [P, 2, NCH])
        st_bf = sb("st_bf", [P, 2, T], BF16)
        xc = sb("xc", [P, NCONV, T])
        xs = sb("xs", [P, 2, KI, T])
        bcm = sb("bcm", [P, 2, T])
        cc = sb("cc", [P, 2, T])
        cz = sb("cz", [P, T])
        sz = sb("sz", [P, 2, KI, T])
        xdt = sb("xdt", [P, NC, DI])
        xw = sb("xw", [P, NC - 1, DI])
        btok = sb("btok", [P, NC, NS])
        gm = sb("gm", [P, T])
        lx = sb("lx", [P, 2, T])
        mx = sb("mx", [P, 4, T])
        es = sb("es", [P, 2, T])
        c2 = sb("c2", [P, 2, T])
        hst = sb("hst", [P, NC - 1, KI, P])
        hs = sb("hs", [P, KI, P])
        yg = sb("yg", [P, 2, KI, T])
        sq = sb("sq", [P, T])
        sqsum = sb("sqsum", [P, T])

        flat = "p a t -> p (a t)"
        NW = DPROJ - NH
        raw_w = [[yg[:, 0].rearrange(flat)[:, 0:NW], yg[:, 1].rearrange(flat)[:, 0:NW]],
                 [xs[:, 1].rearrange(flat)[:, 0:NW], sz[:, 1].rearrange(flat)[:, 0:NW]]]
        wdt = hs[:, 0:KD, :]
        raw_woutT = xdt[:].rearrange("p c (k n) -> p c k n", k=1)[:, :, 0, :]
        raw_wo = xw[:].rearrange("p c n -> p (c n)")[:, 0:4 * D].rearrange("p (m n) -> p m n", m=4)
        raw_ffT = mx[:].rearrange("p c n -> p (c n)")[:, 0:KD * D].rearrange("p (k n) -> p k n", k=KD)
        raw_vrT = mx[0:RANK, 2, 0:D]
        raw_cT = mx[0:RANK, 2, D:2 * D]

        last_squares = xs[:, 0]

        def banks(name, n):
            return [ctx.enter_context(nc.psum_tensor(f"{name}{i}", [P, T], F32)) for i in range(n)]

        pj, sbk, py, mi = banks("pj", 2), banks("sbk", 2), banks("py", 2), banks("mi", 2)

        def ring(name):
            return [sem(f"{name}_full{i}") for i in range(2)], [sem(f"{name}_free{i}") for i in range(2)]

        pj_full, pj_free = ring("pj")
        sb_full, sb_free = ring("sb")
        py_full, py_free = ring("py")
        mi_full, mi_free = ring("mi")

        (passed, i_loaded, c_loaded, v_loaded, f_loaded, setup_done, wdt_hi_ready, wdt_lo_ready, a_exp, x_loaded,
         ln1_stats, ln1_mv, ln1_ve, ln1_rstd, xn_ready, xnt_hi_ready, xres_ready, na_ready, e_ready, u_ready, ln_ready,
         dt_step, r_ready, fin_step, al_ready, s_ready, wd_ready, w_ready, spc_step, spc_ready, conv_first,
         conv_step, bc_ready, xs_ready, xw_ready, m_ready, c2_ready, hs_ready, yg_ready, sq_step,
         sqsum_ready, ms_ready, rms_ready, ln2_stats, ln2_mv, ln2_ve, ln2_rstd, xn2_ready,
         otb_ready, out_stored) = (sem(n) for n in (
            "passed i_loaded c_loaded v_loaded f_loaded setup_done wdt_hi_ready wdt_lo_ready a_exp x_loaded "
            "ln1_stats ln1_mv ln1_ve ln1_rstd xn_ready xnt_hi_ready xres_ready na_ready e_ready u_ready ln_ready "
            "dt_step r_ready fin_step al_ready s_ready wd_ready w_ready spc_step spc_ready conv_first conv_step bc_ready "
            "xs_ready xw_ready m_ready c2_ready hs_ready yg_ready sq_step sqsum_ready ms_ready rms_ready "
            "ln2_stats ln2_mv ln2_ve ln2_rstd xn2_ready otb_ready out_stored").split())

        last_sq = sem("last_sq")
        w_loaded = [sem("w_loaded_f"), sem("w_loaded_b")]
        w_hi_ready = [sem("w_hi_ready_f"), sem("w_hi_ready_b")]
        w_lo_ready = [sem("w_lo_ready_f"), sem("w_lo_ready_b")]
        cc_loaded = [sem("cc_loaded_f"), sem("cc_loaded_b")]

        def pj_use(b, d, t):
            n = NT * d + t
            return n % 2, b * NT + n // 2

        def sb_use(b, d, name):
            n = len(BC) * d + BC.index(name)
            return n % 2, b * len(BC) + n // 2

        def py_use(b, d, p):
            n = KI * d + p
            return n % 2, b * KI + n // 2

        def alone(eng):
            eng.sem_inc(passed, 1)

        block = ctx.enter_context(nc.Block())

        @block.sync
        def _(sp):
            def load_win(d):
                for k in range(KD):
                    sp.dma_start(raw_w[d][k], win[d][P * k:P * k + P, 0:NW]).then_inc(w_loaded[d], 16)

            sp.dma_start(xin[:], x[0].rearrange("(c p) d -> p c d", p=P)).then_inc(x_loaded, 16)
            sp.dma_start(cst[:], consts).then_inc(i_loaded, 16)
            load_win(0)
            for d in range(2):
                sp.dma_start(wdt[:, :, NH * d:NH * d + NH],
                             win[d][:, NW:DPROJ].rearrange("(k p) n -> p k n", p=P)).then_inc(c_loaded, 16)
            sp.dma_start(selc[:], selcol).then_inc(c_loaded, 16)
            for d in range(2):
                sp.dma_start(cw[:, d], convw[d]).then_inc(v_loaded, 16)
                sp.dma_start(cb[:, d], convb[d]).then_inc(v_loaded, 16)
                sp.dma_start(dtb_sb[NH * d:NH * d + NH, :], dtb[d].rearrange("(h o) -> h o", o=1)).then_inc(v_loaded, 16)
                sp.dma_start(arow[:, NH * d:NH * d + NH], alog[d].partition_broadcast(P)).then_inc(v_loaded, 16)
            load_win(1)
            for d in range(2):
                sp.dma_start(nw[:, d], normw[d]).then_inc(f_loaded, 16)
                for e2 in range(2):
                    sp.dma_start(dsk[HP * e2:HP * e2 + HP, d, :],
                                 dskip[d][e2].partition_broadcast(HP)).then_inc(f_loaded, 16)
                sp.dma_start(raw_woutT[:, 2 * d:2 * d + 2, :],
                             woutT[d].rearrange("(m p) n -> p m n", p=P)).then_inc(f_loaded, 16)
            sp.dma_start(raw_wo, wo.rearrange("(m p) n -> p m n", p=P)).then_inc(f_loaded, 16)
            sp.dma_start(raw_ffT, ffT.rearrange("(k p) n -> p k n", p=P)).then_inc(f_loaded, 16)
            sp.dma_start(raw_vrT, vrT).then_inc(f_loaded, 16)
            sp.dma_start(raw_cT, cT).then_inc(f_loaded, 16)
            sp.dma_start(bo_sb[:], bo.partition_broadcast(P)).then_inc(f_loaded, 16)
            sp.dma_start(ffb_sb[:], ffb.partition_broadcast(P)).then_inc(f_loaded, 16)

            def copy_c(b, d):
                sp.wait_ge(bc_ready, 2 * b + d + 1)
                for dst in (cc[0:NS, d, :], cc[NS:P, d, :], cz[0:NS, :]):
                    sp.dma_start(dst, bcm[NS:P, d, :]).then_inc(cc_loaded[d], 16)

            def store(phase, it, b, c):
                bank, used = misc_use(phase, it, f"f{c}")
                sp.wait_ge(mi_free[bank], used + 2)
                alone(sp)
                sp.dma_start(out[b, Q * c:Q * c + Q, :], ot[:, c, :]).then_inc(out_stored, 16)

            def load_x(b):
                sp.wait_ge(xres_ready, b)
                alone(sp)
                sp.dma_start(xin[:], x[b].rearrange("(c p) d -> p c d", p=P)).then_inc(x_loaded, 16)

            copy_c(0, 0)
            copy_c(0, 1)
            def turn(it, more):
                copy_c(it + 1, 0)
                store("loop", it, it, 0)
                store("loop", it, it, 1)
                copy_c(it + 1, 1)
                if more:
                    load_x(it + 2)
                store("loop", it, it, 2)
                store("loop", it, it, 3)

            load_x(1)
            with sp.Fori(0, NB - 2) as it:
                turn(it, True)
            turn(NB - 2, False)
            for c in range(NC):
                store("last", 0, NB - 1, c)
            sp.wait_ge(out_stored, 16 * NC * NB + 1)

        @block.tensor
        def _(pe):
            def misc(phase, it, name):
                bank, used = misc_use(phase, it, name)
                pe.wait_ge(mi_free[bank], used + 1)
                return mi[bank], mi_full[bank]

            def fold_weights(uses):
                for n in uses:
                    ps, full = misc("start", 0, f"w{n}")
                    if n < 2 * KI:
                        d, t = divmod(n, KI)
                        for m in range(KD):
                            mm = pe.matmul(ps[:, 0:D], raw_woutT[:, 2 * d + m, P * t:P * t + P], raw_wo[:, 2 * d + m, :],
                                           start=(m == 0), stop=(m == KD - 1))
                    else:
                        for k in range(KD):
                            mm = pe.matmul(ps[:, D * k:D * k + D], raw_vrT[:, P * k:P * k + P], raw_cT, start=True, stop=True)
                    mm.then_inc(full, 1)

            def norm_transposed(phase, it, b):
                pe.wait_ge(xn_ready, NC * b + NC)
                for k in range(KD):
                    ps, full = misc(phase, it, f"a{k}")
                    for c in range(NC):
                        mm = pe.transpose(ps[:, Q * c:Q * c + Q], xn[:, c, P * k:P * k + P], ident)
                    mm.then_inc(full, 1)

            def released(phase, it, name):
                bank, used = misc_use(phase, it, name)
                pe.wait_ge(mi_free[bank], used + 2)

            def wait_xnt(phase, it):
                for k in range(KD):
                    released(phase, it, f"a{k}")
                alone(pe)

            def three_passes(ps, hi, lo):
                for k in range(KD):
                    pe.matmul(ps[:], hi(k), xnt_hi[:, k, :], start=(k == 0), stop=False)
                    pe.matmul(ps[:], hi(k), xnt_lo[:, k, :], start=False, stop=False)
                    mm = pe.matmul(ps[:], lo(k), xnt_hi[:, k, :], start=False, stop=(k == KD - 1))
                return mm

            def project(b, d, t):
                bank, used = pj_use(b, d, t)
                pe.wait_ge(pj_free[bank], used + 1)
                c0 = COLS[t]
                three_passes(pj[bank], lambda k: w_hi[:, d, k, c0:c0 + P],
                             lambda k: w_lo[:, d, k, c0:c0 + P]).then_inc(pj_full[bank], 1)

            def dt_project(phase, it):
                ps, full = misc(phase, it, "dtm")
                three_passes(ps, lambda k: wdt_hi[:, k, :], lambda k: wdt_lo[:, k, :]).then_inc(full, 1)

            def dt_transposed(phase, it):
                released(phase, it, "dtm")
                alone(pe)
                ps, full = misc(phase, it, "dtt")
                alone(pe)
                for c in range(NC):
                    mm = pe.transpose(ps[:, 2 * NH * c:2 * NH * (c + 1)], dt_t[:, Q * c:Q * c + Q], ident[0:2 * NH, 0:2 * NH])
                mm.then_inc(full, 1)

            def sums(phase, it, b, d):
                pe.wait_ge(al_ready, 2 * b + d + 1)
                ps, full = misc(phase, it, f"{d}S")
                av = al[:, d].rearrange("p c h -> p (c h)")
                pe.matmul(ps[:, 0:NCH], tri[d], av, start=True, stop=True)
                pe.matmul(ps[:, NCH:2 * NCH], ones, av, start=True, stop=True).then_inc(full, 1)

            def s_transposed(phase, it, b, d):
                pe.wait_ge(spc_ready, 2 * b + d + 1)
                ps, full = misc(phase, it, f"{d}ST")
                alone(pe)
                pb = ps[:, 0:T // 2].bitcast(BF16)
                for c in range(NC):
                    mm = pe.transpose(pb[:, Q * c:Q * c + Q], spc[:, c, :], identb[:])
                mm.then_inc(full, 1)

            def spread(b, d, name):
                bank, used = sb_use(b, d, name)
                pe.wait_ge(sb_free[bank], used + 1)
                n = int(name[1])
                if name[0] == "p":
                    mm = pe.matmul(sbk[bank][:, LATER[d]], selp[:, 2 * n:2 * n + 2, :], st_bf[:, d, LATER[d]],
                                   start=True, stop=True)
                else:
                    pe.matmul(sbk[bank][:], sel[:, n, :], st_bf[:, d, :], start=True, stop=False)
                    mm = pe.matmul(sbk[bank][:], identb[:], hide[:, d, :].unsqueeze(1).broadcast_to([P, NC, Q]),
                                   start=False, stop=True)
                mm.then_inc(sb_full[bank], 1)

            def b_tokens(phase, it, d):
                ps, full = misc(phase, it, f"{d}bt")
                for c in range(NC):
                    mm = pe.transpose(ps[:, P * c:P * c + P], bcm[:, d, Q * c:Q * c + Q], ident)
                mm.then_inc(full, 1)

            def x_tokens(phase, it, d, j):
                ps, full = misc(phase, it, f"{d}x{j}")
                c = ORDER[d][j]
                for t in range(KI):
                    mm = pe.transpose(ps[:, P * t:P * t + P], xs[:, d, t, Q * c:Q * c + Q], ident)
                mm.then_inc(full, 1)

            def scores(phase, it, b, d):
                pe.wait_ge(cc_loaded[d], 48 * (b + 1))
                ps, full = misc(phase, it, f"{d}g")
                for c in range(NC):
                    mm = pe.matmul(ps[:, Q * c:Q * c + Q], bcm[:, d, Q * c:Q * c + Q], cz[:, Q * c:Q * c + Q],
                                   start=True, stop=True)
                mm.then_inc(full, 1)

            def state(phase, it, b, d, j):
                u = 2 * b + d
                if j == 0:
                    released(phase, it, f"{d}bt")
                pe.wait_ge(xw_ready, (NC - 1) * u + j + 1)
                ps, full = misc(phase, it, f"{d}s{j}")
                heads = xw[:, j, :].rearrange("p (r e q) -> p e r q", e=2, q=HP)
                for half in range(2):
                    mm = pe.matmul(ps[NS * half:NS * half + NS, 0:DI // 2].rearrange("p (r q) -> p r q", q=HP),
                                   btok[:, ORDER[d][j], :], heads[:, half], start=True, stop=True, skip_group_check=True)
                mm.then_inc(full, 1)

            def outputs(phase, it, b, d, p):
                u = 2 * b + d
                bank, used = py_use(b, d, p)
                pe.wait_ge(py_free[bank], used + 1)
                pe.wait_ge(m_ready, 2 + NH * u + 2 * p + 2)
                for c in range(NC):
                    for half in range(2):
                        h = 2 * p + half
                        pe.matmul(py[bank][HP * half:HP * half + HP, Q * c:Q * c + Q], xdt[:, c, HP * h:HP * h + HP],
                                  mx[:, h % 4, Q * c:Q * c + Q], start=(c == 0), stop=False, skip_group_check=True)
                if p == 0:
                    released(phase, it, f"{d}s{NC - 2}")
                pe.wait_ge(c2_ready, 2 + KI * u + p + 1)
                for j in range(NC - 1):
                    c = ORDER[d][j + 1]
                    mm = pe.matmul(py[bank][:, Q * c:Q * c + Q], hst[:, j, p, :], c2[:, p % 2, Q * c:Q * c + Q],
                                   start=False, stop=(j == NC - 2), skip_group_check=True)
                mm.then_inc(py_full[bank], 1)

            def squares(phase, it, b, d):
                pe.wait_ge(sqsum_ready, 2 * b + d + 1)
                ps, full = misc(phase, it, f"{d}ss")
                for c in range(NC):
                    mm = pe.matmul(ps[:, c:c + 1], sqsum[:, Q * c:Q * c + Q], ones[:, 0:1], start=True, stop=True)
                mm.then_inc(full, 1)

            def mix(phase, it, b, d, half):
                if half == 0:
                    pe.wait_ge(yg_ready, KI * (2 * b + d + 1))
                ps, full = misc(phase, it, f"{d}o{half}")
                for i in range(2):
                    c = 2 * half + i
                    for t in range(KI):
                        mm = pe.matmul(ps[:, D * i:D * i + D], yg[:, d, t, Q * c:Q * c + Q], wc[:, d, t, :],
                                       start=(t == 0), stop=(t == KI - 1))
                mm.then_inc(full, 1)

            def last_mix(b):
                ps, full = zip(*(misc("last", 0, f"1o{half}") for half in range(2)))
                bank, used = pj_use(NB, 0, 0)
                pe.wait_ge(pj_free[bank], used + 1)

                def mixed(t):
                    pe.wait_ge(yg_ready, KI * (2 * b + 1) + t + 1)
                    for c in range(NC):
                        i, half = c % 2, c // 2
                        mm = pe.matmul(ps[half][:, D * i:D * i + D], yg[:, 1, t, Q * c:Q * c + Q], wc[:, 1, t, :],
                                       start=(t == i == 0), stop=(t == KI - 1), skip_group_check=True)
                        if t == KI - 1 and i == 1:
                            mm.then_inc(full[half], 1)

                def square_sums(t):
                    pe.wait_ge(last_sq, t + 1)
                    for c in range(NC):
                        mm = pe.matmul(pj[bank][:, c:c + 1], last_squares[:, t, Q * c:Q * c + Q], ones[:, 0:1],
                                       start=(t == c == 0), stop=(t == KI - 1), skip_group_check=True)
                    return mm

                for t in range(KI - 1):
                    mixed(t)
                    square_sums(t)
                square_sums(KI - 1).then_inc(pj_full[bank], 1)
                mixed(KI - 1)

            def norm2_transposed(phase, it, b, c):
                pe.wait_ge(xn2_ready, NC * b + c + 1)
                ps, full = misc(phase, it, f"t{c}")
                for k in range(KD):
                    mm = pe.transpose(ps[:, P * k:P * k + P], xn2[:, c, P * k:P * k + P], ident)
                mm.then_inc(full, 1)

            def feed(phase, it, c):
                released(phase, it, f"t{c}")
                ps, full = misc(phase, it, f"f{c}")
                for k in range(KD):
                    mm = pe.matmul(ps[:, 0:D], xn2t[:, c % 2, k, :], wff[:, k, :], start=(k == 0), stop=(k == KD - 1))
                mm.then_inc(full, 1)

            def scan_start(phase, it, b, d):
                pe.wait_ge(bc_ready, 2 * b + d + 1)
                b_tokens(phase, it, d)
                pe.wait_ge(xs_ready, KI * (2 * b + d + 1))
                x_tokens(phase, it, d, 0)
                x_tokens(phase, it, d, 1)
                if d == 0:
                    s_transposed(phase, it, b, 0)
                project(b, d, NT - 1)
                x_tokens(phase, it, d, 2)
                x_tokens(phase, it, d, 3)
                if d == 0:
                    released(phase, it, "0ST")
                spread(b, d, "h0")
                spread(b, d, "h1")

            def reversed_scan(phase, it, b, nxt):
                more = phase == "loop"
                scan_start(phase, it, b, 1)
                scores(phase, it, b, 1)
                spread(b, 1, "p0")
                if more:
                    norm_transposed(phase, it, nxt)
                spread(b, 1, "h2")
                state(phase, it, b, 1, 0)
                spread(b, 1, "h3")
                state(phase, it, b, 1, 1)
                if more:
                    wait_xnt(phase, it)
                    dt_project(phase, it)
                    project(nxt, 0, 0)
                squares(phase, it, b, 0)
                spread(b, 1, "p1")
                spread(b, 1, "h4")
                state(phase, it, b, 1, 2)
                mix(phase, it, b, 0, 0)
                if more:
                    project(nxt, 0, 1)
                outputs(phase, it, b, 1, 0)
                if more:
                    project(nxt, 0, 2)
                    dt_transposed(phase, it)
                spread(b, 1, "h5")
                spread(b, 1, "p2")
                mix(phase, it, b, 0, 1)
                if more:
                    project(nxt, 0, 3)
                spread(b, 1, "h6")
                spread(b, 1, "h7")
                outputs(phase, it, b, 1, 1)
                spread(b, 1, "p3")
                if more:
                    project(nxt, 0, 4)
                outputs(phase, it, b, 1, 2)
                outputs(phase, it, b, 1, 3)
                if more:
                    project(nxt, 0, 5)
                    project(nxt, 0, 6)
                    sums(phase, it, nxt, 0)
                    project(nxt, 0, 7)

            def forward_scan(phase, it, b, last):
                more = phase == "loop"
                scan_start(phase, it, b, 0)
                project(b, 1, 0)
                scores(phase, it, b, 0)
                spread(b, 0, "p0")
                spread(b, 0, "h2")
                state(phase, it, b, 0, 0)
                spread(b, 0, "h3")
                state(phase, it, b, 0, 1)
                project(b, 1, 1)
                if more:
                    squares(phase, it, last, 1)
                spread(b, 0, "p1")
                spread(b, 0, "h4")
                state(phase, it, b, 0, 2)
                sums(phase, it, b, 1)
                if more:
                    mix(phase, it, last, 1, 0)
                outputs(phase, it, b, 0, 0)
                project(b, 1, 2)
                spread(b, 0, "h5")
                spread(b, 0, "p2")
                if more:
                    mix(phase, it, last, 1, 1)
                spread(b, 0, "h6")
                spread(b, 0, "h7")
                outputs(phase, it, b, 0, 1)
                s_transposed(phase, it, b, 1)
                outputs(phase, it, b, 0, 2)
                spread(b, 0, "p3")
                if more:
                    norm2_transposed(phase, it, last, 0)
                    norm2_transposed(phase, it, last, 1)
                project(b, 1, 3)
                if more:
                    feed(phase, it, 0)
                    feed(phase, it, 1)
                project(b, 1, 4)
                if more:
                    norm2_transposed(phase, it, last, 2)
                    norm2_transposed(phase, it, last, 3)
                outputs(phase, it, b, 0, 3)
                project(b, 1, 5)
                if more:
                    feed(phase, it, 2)
                    feed(phase, it, 3)
                project(b, 1, 6)
                project(b, 1, 7)
                released(phase, it, "1ST")

            pe.wait_ge(i_loaded, 16)
            norm_transposed("start", 0, 0)
            wait_xnt("start", 0)
            pe.wait_ge(w_lo_ready[0], KD)
            project(0, 0, 0)
            pe.wait_ge(wdt_lo_ready, 1)
            dt_project("start", 0)
            project(0, 0, 1)
            dt_transposed("start", 0)
            project(0, 0, 2)
            pe.wait_ge(f_loaded, 16 * 14)
            fold_weights([0, 1])
            project(0, 0, 3)
            fold_weights([2, 3])
            project(0, 0, 4)
            fold_weights([4, 5, 6, 7])
            project(0, 0, 5)
            sums("start", 0, 0, 0)
            fold_weights([8])
            project(0, 0, 6)
            project(0, 0, 7)
            pe.wait_ge(w_lo_ready[1], KD)
            forward_scan("start", 0, 0, None)

            with pe.Fori(0, NB - 1) as it:
                reversed_scan("loop", it, it, it + 1)
                forward_scan("loop", it, it + 1, it)

            b = NB - 1
            reversed_scan("last", 0, b, None)
            last_mix(b)
            for c0 in (0, 2):
                for c in (c0, c0 + 1):
                    norm2_transposed("last", 0, b, c)
                for c in (c0, c0 + 1):
                    feed("last", 0, c)

        @block.scalar
        def _(act):
            def misc(phase, it, name):
                bank, used = misc_use(phase, it, name)
                act.wait_ge(mi_full[bank], used + 1)
                return mi[bank], mi_free[bank]

            def split_high(d):
                act.wait_ge(w_loaded[d], 16 * KD)
                for k in range(KD):
                    nc.scalar.activation(w_hi[:, d, k, :], raw_w[d][k], ACT.Copy).then_inc(w_hi_ready[d], 1)

            def split_dt_high():
                act.wait_ge(c_loaded, 16 * 3)
                act.wait_ge(setup_done, 1)
                nc.scalar.activation(wdt_hi[:], wdt, ACT.Copy).then_inc(wdt_hi_ready, 1)
                act.wait_ge(v_loaded, 16 * 8)
                nc.scalar.activation(arow[:], arow[:], ACT.Exp).then_inc(a_exp, 1)

            def fold_weights(uses):
                for n in uses:
                    d, t = divmod(n, KI)
                    ps, free = misc("start", 0, f"w{n}")
                    nc.scalar.activation(wc[:, d, t, :], ps[:, 0:D], ACT.Copy, scale=nw[:, d, t:t + 1]).then_inc(free, 1)

            def norm_high(phase, it):
                for k in range(KD):
                    ps, _ = misc(phase, it, f"a{k}")
                    nc.scalar.activation(xnt_hi[:, k, :], ps[:], ACT.Copy).then_inc(xnt_hi_ready, 1)

            def dt_bias(phase, it):
                if phase == "loop":
                    act.wait_ge(out_stored, 16 * NC * it + 1)
                ps, free = misc(phase, it, "dtm")
                nc.scalar.activation(dt_t, ps[0:2 * NH, :], ACT.Identity, bias=dtb_sb[:, 0:1]).then_inc(free, 1)

            def soft_exp(b):
                act.wait_ge(na_ready, b + 1)
                nc.scalar.activation(e[:], na[:], ACT.Exp).then_inc(e_ready, 1)

            def soft_log(b):
                act.wait_ge(u_ready, b + 1)
                nc.scalar.activation(lnu[:], u1[:], ACT.Ln).then_inc(ln_ready, 1)

            def s_pieces(phase, it, d):
                ps, free = misc(phase, it, f"{d}ST")
                nc.scalar.activation(st_bf[:, d, :], ps[:, 0:T // 2].bitcast(BF16), ACT.Copy).then_inc(free, 1)

            def conv_start(b, d, t):
                bank, used = pj_use(b, d, t)
                u = 2 * b + d
                if t == 0 and not (isinstance(b, int) and b == d == 0):
                    act.wait_ge(xs_ready, KI * u)
                act.wait_ge(pj_full[bank], used + 1)
                nc.scalar.activation(xc[:, t, :], pj[bank][:], ACT.Identity, bias=cb[:, d, t:t + 1],
                                     scale=cw[:, d, t, KW - 1:KW]).then_inc(conv_first, 1)

            def conv_end(b, d, t):
                bank, used = pj_use(b, d, t)
                if t == 0 and not (isinstance(b, int) and b == 0):
                    act.wait_ge(yg_ready, KI * (2 * b + d - 1))
                act.wait_ge(pj_free[bank], used + 2)
                dst, ready = (bcm[:, d, :], bc_ready) if t == 0 else (xs[:, d, t - 1, :], xs_ready)
                nc.scalar.activation(dst, xc[:, t, :], ACT.Silu).then_inc(ready, 1)

            def gate(b, d, t):
                bank, used = pj_use(b, d, t)
                act.wait_ge(pj_full[bank], used + 1)
                nc.scalar.activation(sz[:, d, t - NCONV, :], pj[bank][:], ACT.Silu).then_inc(pj_free[bank], 1)

            def decays(b, d):
                act.wait_ge(wd_ready, 2 * b + d + 1)
                nc.scalar.activation(w_end[:, d], wd[:, d], ACT.Exp)
                nc.scalar.activation(e_end[:, d], s_all[:, d, 1].rearrange("p c h -> p (c h)"), ACT.Exp).then_inc(w_ready, 1)

            def spread(b, d, name):
                u = 2 * b + d
                bank, used = sb_use(b, d, name)
                n = int(name[1])
                act.wait_ge(sb_full[bank], used + 1)
                if name[0] == "h":
                    act.wait_ge(m_ready, NH * u + n + 1)
                    for c in range(NC):
                        o = c * NH + n
                        i = nc.scalar.activation(lx[:, n % 2, Q * c:Q * c + Q], sbk[bank][:, Q * c:Q * c + Q], ACT.Exp,
                                                 bias=neg_s[:, d, o:o + 1])
                    i.then_inc(sb_free[bank], 1)
                else:
                    act.wait_ge(c2_ready, KI * u + n + 1)
                    nc.scalar.activation(es[:, n % 2, LATER[d]], sbk[bank][:, LATER[d]], ACT.Exp).then_inc(sb_free[bank], 1)

            def b_tokens(phase, it, d):
                ps, free = misc(phase, it, f"{d}bt")
                src = ps[:].rearrange("p (c n) -> p c n", c=NC)[:, :, 0:NS]
                nc.scalar.activation(btok[:], src, ACT.Copy).then_inc(free, 1)

            def norm2(phase, it, c):
                ps, free = misc(phase, it, f"t{c}")
                nc.scalar.activation(xn2t[:, c % 2], ps[:, 0:D].rearrange("p (k n) -> p k n", k=KD), ACT.Copy).then_inc(free, 1)

            def spreads(b, d, *names):
                for name in names:
                    spread(b, d, name)

            def conv_ends(b, d, *tiles):
                for t in tiles:
                    conv_end(b, d, t)

            def gates(b, d, *tiles):
                for t in tiles:
                    gate(b, d, t)

            def scan_start(phase, it, b, d):
                b_tokens(phase, it, d)
                if d == 0:
                    s_pieces(phase, it, 0)
                gates(b, d, NT - 1)
                decays(b, d)
                spreads(b, d, "h0", "h1")
                if d == 1 and phase == "loop":
                    norm_high(phase, it)

            def reversed_scan(phase, it, b, nxt):
                more = phase == "loop"
                scan_start(phase, it, b, 1)
                spreads(b, 1, "p0", "h2", "h3")
                if more:
                    dt_bias(phase, it)
                    conv_start(nxt, 0, 0)
                spreads(b, 1, "p1", "h4")
                if more:
                    conv_start(nxt, 0, 1)
                    conv_start(nxt, 0, 2)
                    soft_exp(nxt)
                spreads(b, 1, "h5", "p2")
                if more:
                    conv_start(nxt, 0, 3)
                spreads(b, 1, "h6", "h7", "p3")
                if more:
                    soft_log(nxt)
                    conv_start(nxt, 0, 4)
                    conv_ends(nxt, 0, 0, 1, 2, 3, 4)
                    gates(nxt, 0, 5, 6, 7)

            def forward_scan(phase, it, b):
                more = phase == "loop"
                scan_start(phase, it, b, 0)
                spreads(b, 0, "p0", "h2", "h3")
                conv_start(b, 1, 0)
                spreads(b, 0, "p1", "h4")
                conv_start(b, 1, 1)
                conv_start(b, 1, 2)
                spreads(b, 0, "h5", "p2", "h6", "h7")
                s_pieces(phase, it, 1)
                spreads(b, 0, "p3")
                if more:
                    norm2(phase, it, 0)
                    norm2(phase, it, 1)
                conv_start(b, 1, 3)
                conv_ends(b, 1, 0, 1, 2)
                conv_start(b, 1, 4)
                if more:
                    norm2(phase, it, 2)
                    norm2(phase, it, 3)
                conv_ends(b, 1, 3, 4)
                gates(b, 1, 5, 6, 7)

            split_high(0)
            norm_high("start", 0)
            split_dt_high()
            conv_start(0, 0, 0)
            dt_bias("start", 0)
            conv_start(0, 0, 1)
            soft_exp(0)
            conv_start(0, 0, 2)
            soft_log(0)
            fold_weights([0, 1])
            conv_start(0, 0, 3)
            fold_weights([2, 3])
            conv_start(0, 0, 4)
            conv_ends(0, 0, 0, 1, 2)
            fold_weights([4, 5, 6, 7])
            split_high(1)
            conv_ends(0, 0, 3, 4)
            gates(0, 0, 5, 6, 7)
            forward_scan("start", 0, 0)

            with act.Fori(0, NB - 1) as it:
                reversed_scan("loop", it, it, it + 1)
                forward_scan("loop", it, it + 1)

            reversed_scan("last", 0, NB - 1, None)
            for t in range(KI):
                act.wait_ge(yg_ready, KI * (2 * NB - 1) + t + 1)
                nc.scalar.activation(last_squares[:, t, :], yg[:, 1, t, :], ACT.Square).then_inc(last_sq, 1)
            for c in range(NC):
                norm2("last", 0, c)

        @block.vector
        def _(dve):
            for s in (*pj_free, *sb_free, *py_free, *mi_free):
                dve.sem_inc(s, 1)
            for s in (m_ready, c2_ready):
                dve.sem_inc(s, 2)
            dve.sem_inc(out_stored, 1)

            def misc(phase, it, name):
                bank, used = misc_use(phase, it, name)
                dve.wait_ge(mi_full[bank], used + 1)
                return mi[bank], mi_free[bank]

            def setup():
                dve.memset(wdt[:, :, 2 * NH:P], 0.0)
                dve.memset(halves[:], -0.5).then_inc(setup_done, 1)

            def zeros():
                dve.memset(spc[:], 0.0)
                dve.memset(cz[NS:P, :], 0.0)
                dve.memset(hst[:], 0.0).then_inc(setup_done, 1)

            def selectors():
                dve.wait_ge(i_loaded, 16)
                dve.wait_ge(c_loaded, 16 * 3)
                dve.tensor_copy(identb[:], ident)
                for d in range(2):
                    dve.tensor_scalar(hide[:, d, :], tri[d], -FAR, FAR, ALU.mult, ALU.add)
                dve.tensor_copy(sel[:], selc[:].unsqueeze(2).broadcast_to([P, NH, P]))
                dve.tensor_copy(selp[:], selc[:].unsqueeze(2).broadcast_to([P, NH, HP]))

            def split_low(d):
                for k in range(KD):
                    dve.wait_ge(w_hi_ready[d], k + 1)
                    dve.tensor_tensor(w_lo[:, d, k, :], raw_w[d][k], w_hi[:, d, k, :].bitcast(F32),
                                      ALU.subtract).then_inc(w_lo_ready[d], 1)

            def split_dt_low():
                dve.wait_ge(wdt_hi_ready, 1)
                dve.tensor_tensor(wdt_lo[:], wdt, wdt_hi[:].bitcast(F32), ALU.subtract).then_inc(wdt_lo_ready, 1)
                dve.wait_ge(a_exp, 1)
                dve.tensor_scalar(abc[:], arow[:].unsqueeze(1).broadcast_to([P, NC, 2 * NH]), -1.0, None,
                                  ALU.mult)

            def fold_ffn():
                ps, free = misc("start", 0, f"w{2 * KI}")
                dve.tensor_tensor(wff[:], ps[:].rearrange("p (k n) -> p k n", k=KD), raw_ffT, ALU.add).then_inc(free, 1)

            def norm_stats(src, st, mv, stats, aggr, b):
                for c in range(NC):
                    dve.bn_stats(st[:, c, :], src[:, c, :]).then_inc(stats, 1)
                for c in range(NC):
                    dve.wait_ge(stats, NC * b + c + 1)
                    alone(dve)
                    dve.bn_aggr(mv[:, c, :], st[:, c, :]).then_inc(aggr, 1)

            def norm_scale(dst, src, mv, rstd, ready):
                for c in range(NC):
                    dve.tensor_scalar(dst[:, c, :], src[:, c, :], mv[:, c, 0:1], rstd[:, c:c + 1],
                                      ALU.subtract, ALU.mult).then_inc(ready, 1)

            def norm1_stats(b):
                dve.wait_ge(x_loaded, 16 * (b + 1))
                norm_stats(xin, st1, mv1, ln1_stats, ln1_mv, b)

            def norm1_scale(b):
                dve.wait_ge(ln1_rstd, b + 1)
                norm_scale(xn, xin, mv1, rstd1, xn_ready)

            def norm_low(phase, it, b):
                for k in range(KD):
                    ps, free = misc(phase, it, f"a{k}")
                    dve.wait_ge(xnt_hi_ready, KD * b + k + 1)
                    dve.tensor_tensor(xnt_lo[:, k, :], ps[:], xnt_hi[:, k, :].bitcast(F32), ALU.subtract).then_inc(free, 1)

            def soft_in(phase, it, b):
                ps, free = misc(phase, it, "dtt")
                dve.tensor_copy(v[:].rearrange("p c n -> p (c n)"), ps[:, 0:2 * NCH]).then_inc(free, 1)
                bank, used = misc_use(phase, it, "dtt")
                dve.wait_ge(free, used + 2)
                dve.scalar_tensor_tensor(na[:], v[:], -1.0, v[:], ALU.mult, ALU.min).then_inc(na_ready, 1)

            def soft_mid(b):
                dve.wait_ge(e_ready, b + 1)
                dve.tensor_scalar(u1[:], e[:], 1.0, None, ALU.add).then_inc(u_ready, 1)
                dve.wait_ge(u_ready, b + 1)
                dve.tensor_scalar(du[:], u1[:], -1.0, None, ALU.add).then_inc(dt_step, 1)
                dve.wait_ge(dt_step, 5 * b + 1)
                dve.scalar_tensor_tensor(dd[:], du[:], 0.0, du[:], ALU.is_equal, ALU.add).then_inc(dt_step, 1)
                dve.wait_ge(dt_step, 5 * b + 2)
                dve.reciprocal(rq[:], dd[:]).then_inc(dt_step, 1)

            def soft_out(b):
                dve.wait_ge(ln_ready, b + 1)
                dve.wait_ge(dt_step, 5 * b + 3)
                dve.tensor_tensor(r1[:], lnu[:], rq[:], ALU.mult).then_inc(dt_step, 1)
                dve.wait_ge(dt_step, 5 * b + 4)
                dve.scalar_tensor_tensor(r2[:], du[:], 0.0, r1[:], ALU.is_equal, ALU.add).then_inc(dt_step, 1)
                dve.wait_ge(dt_step, 5 * b + 5)
                dve.tensor_tensor(r3[:], r2[:], e[:], ALU.mult).then_inc(r_ready, 1)

            def dt_values(b, d):
                u = 2 * b + d
                cols = slice(NH * d, NH * d + NH)
                dve.wait_ge(r_ready, b + 1)
                dve.scalar_tensor_tensor(dt[:, d], v[:, :, cols], 0.0, r3[:, :, cols], ALU.max, ALU.add).then_inc(fin_step, 1)
                dve.wait_ge(fin_step, 2 * u + 1)
                dve.tensor_tensor(adt[:, d], dt[:, d], abc[:, :, cols], ALU.mult).then_inc(fin_step, 1)
                dve.wait_ge(fin_step, 2 * u + 2)
                dve.tensor_scalar(al[:, d], adt[:, d], A_FLOOR, None, ALU.max).then_inc(al_ready, 1)

            def s_values(phase, it, b, d):
                ps, free = misc(phase, it, f"{d}S")
                _, used = misc_use(phase, it, f"{d}S")
                dve.tensor_copy(s_all[:, d].rearrange("p s c h -> p (s c h)"), ps[:, 0:2 * NCH]).then_inc(free, 1)
                dve.wait_ge(free, used + 2)
                s, end = (s_all[:, d, i].rearrange("p c h -> p (c h)") for i in range(2))
                dve.tensor_scalar(neg_s[:, d], s, -1.0, None, ALU.mult).then_inc(s_ready, 1)
                dve.tensor_tensor(wd[:, d], end, s, ALU.subtract).then_inc(wd_ready, 1)

            def conv(b, d, t):
                u = 2 * b + d
                bank, used = pj_use(b, d, t)
                dve.wait_ge(conv_first, NCONV * u + t + 1)
                for s in range(1, KW):
                    to = slice(s, T) if d == 0 else slice(0, T - s)
                    of = slice(0, T - s) if d == 0 else slice(s, T)
                    if s > 1:
                        dve.wait_ge(conv_step, (KW - 2) * (NCONV * u + t) + s - 1)
                    i = dve.scalar_tensor_tensor(xc[:, t, to], pj[bank][:, of], cw[:, d, t, KW - 1 - s:KW - s],
                                                 xc[:, t, to], ALU.mult, ALU.add)
                    i.then_inc(pj_free[bank] if s == KW - 1 else conv_step, 1)

            def x_tokens(phase, it, d, j):
                ps, free = misc(phase, it, f"{d}x{j}")
                c = ORDER[d][j]
                dve.tensor_tensor(xdt[:, c, :].rearrange("p (h q) -> p h q", h=NH), ps[:].rearrange("p (h q) -> p h q", h=NH),
                                  dt[:, d, c, :].unsqueeze(2).broadcast_to([P, NH, HP]), ALU.mult).then_inc(free, 1)

            def scores(phase, it, b, d):
                ps, free = misc(phase, it, f"{d}g")
                dve.tensor_copy(gm[:], ps[:]).then_inc(free, 1)

            def weights(phase, it, b, d, h):
                u = 2 * b + d
                if h == 0:
                    bank, used = misc_use(phase, it, f"{d}g")
                    dve.wait_ge(mi_free[bank], used + 2)
                bank, used = sb_use(b, d, f"h{h}")
                dve.wait_ge(sb_free[bank], used + 2)
                dve.tensor_tensor(mx[:, h % 4, :], lx[:, h % 2, :], gm[:], ALU.mult).then_inc(m_ready, 1)

            def state(phase, it, b, d, j):
                u = 2 * b + d
                ps, free = misc(phase, it, f"{d}s{j}")
                if j:
                    dve.wait_ge(hs_ready, (NC - 2) * u + j)
                view = ps[:, 0:DI // 2].rearrange("p (r q) -> p r q", q=HP)
                for half in range(2):
                    lanes, cols = slice(HP * half, HP * half + HP), slice(HP * half, HP * half + HP)
                    if j == 0:
                        i = dve.tensor_copy(hst[lanes, j, :, cols], view[lanes])
                    else:
                        i = dve.tensor_tensor(hst[lanes, j, :, cols], view[lanes], hs[lanes, :, cols], ALU.add)
                i.then_inc(free, 1)

            def outputs(b, d, p):
                u = 2 * b + d
                bank, used = py_use(b, d, p)
                dve.wait_ge(py_full[bank], used + 1)
                dve.scalar_tensor_tensor(yg[:, d, p, :], xs[:, d, p, :], dsk[:, d, p:p + 1], py[bank][:], ALU.mult,
                                         ALU.add).then_inc(py_free[bank], 1)

            def gate(b, d, p):
                bank, used = py_use(b, d, p)
                dve.wait_ge(py_free[bank], used + 2)
                dve.tensor_tensor(yg[:, d, p, :], yg[:, d, p, :], sz[:, d, p, :], ALU.mult).then_inc(yg_ready, 1)

            def squares(phase, it, d):
                ps, free = misc(phase, it, f"{d}ss")
                dve.tensor_copy(ss[:, d, :], ps[:, 0:NC]).then_inc(free, 1)

            def mix(phase, it, b, d, half):
                ps, free = misc(phase, it, f"{d}o{half}")
                if half == 0:
                    dve.wait_ge(xres_ready, b + 1)
                    dve.wait_ge(rms_ready, 2 * b + d + 1)
                for i in range(2):
                    c = 2 * half + i
                    mm = dve.scalar_tensor_tensor(xres[:, c, :], ps[:, D * i:D * i + D], rms[:, d, c:c + 1], xres[:, c, :],
                                                  ALU.mult, ALU.add)
                mm.then_inc(free, 1)

            def norm2_stats(phase, it, b):
                for half in range(2):
                    bank, used = misc_use(phase, it, f"1o{half}")
                    dve.wait_ge(mi_free[bank], used + 2)
                norm_stats(xres, st2, mv2, ln2_stats, ln2_mv, b)

            def norm2_scale(b):
                dve.wait_ge(ln2_rstd, b + 1)
                norm_scale(xn2, xres, mv2, rstd2, xn2_ready)

            def feed(phase, it, b, c):
                ps, free = misc(phase, it, f"f{c}")
                if c == 0:
                    dve.wait_ge(otb_ready, b + 1)
                dve.tensor_tensor(ot[:, c, :], ps[:, 0:D], ot[:, c, :], ALU.add).then_inc(free, 1)

            def tokens(phase, it, d, *chunks):
                for j in chunks:
                    x_tokens(phase, it, d, j)

            def reversed_scan(phase, it, b, nxt):
                more = phase == "loop"

                def w(*heads):
                    for h in heads:
                        weights(phase, it, b, 1, h)

                if more:
                    norm1_stats(nxt)
                tokens(phase, it, 1, 0, 1, 2)
                if more:
                    norm1_scale(nxt)
                tokens(phase, it, 1, 3)
                scores(phase, it, b, 1)
                w(0)
                if more:
                    norm_low(phase, it, nxt)
                w(1)
                state(phase, it, b, 1, 0)
                w(2)
                state(phase, it, b, 1, 1)
                squares(phase, it, 0)
                w(3)
                state(phase, it, b, 1, 2)
                if more:
                    conv(nxt, 0, 0)
                mix(phase, it, b, 0, 0)
                if more:
                    conv(nxt, 0, 1)
                outputs(b, 1, 0)
                if more:
                    soft_in(phase, it, nxt)
                else:
                    gate(b, 1, 0)
                w(4)
                if more:
                    conv(nxt, 0, 2)
                mix(phase, it, b, 0, 1)
                w(5)
                if more:
                    conv(nxt, 0, 3)
                outputs(b, 1, 1)
                if not more:
                    gate(b, 1, 1)
                if more:
                    soft_mid(nxt)
                w(6, 7)
                outputs(b, 1, 2)
                if more:
                    conv(nxt, 0, 4)
                    soft_out(nxt)
                    dt_values(nxt, 0)
                    s_values(phase, it, nxt, 0)
                else:
                    gate(b, 1, 2)
                outputs(b, 1, 3)
                if not more:
                    gate(b, 1, 3)

            def forward_scan(phase, it, b, last):
                more = phase == "loop"

                def w(*heads):
                    for h in heads:
                        weights(phase, it, b, 0, h)

                tokens(phase, it, 0, *range(NC))
                dt_values(b, 1)
                scores(phase, it, b, 0)
                w(0, 1)
                state(phase, it, b, 0, 0)
                w(2)
                state(phase, it, b, 0, 1)
                if more:
                    squares(phase, it, 1)
                w(3)
                state(phase, it, b, 0, 2)
                conv(b, 1, 0)
                s_values(phase, it, b, 1)
                conv(b, 1, 1)
                if more:
                    mix(phase, it, last, 1, 0)
                outputs(b, 0, 0)
                w(4)
                conv(b, 1, 2)
                if more:
                    mix(phase, it, last, 1, 1)
                w(5)
                if more:
                    norm2_stats(phase, it, last)
                outputs(b, 0, 1)
                if more:
                    norm2_scale(last)
                w(6, 7)
                outputs(b, 0, 2)
                if more:
                    feed(phase, it, last, 0)
                    feed(phase, it, last, 1)
                conv(b, 1, 3)
                outputs(b, 0, 3)
                conv(b, 1, 4)
                if more:
                    feed(phase, it, last, 2)
                    feed(phase, it, last, 3)

            setup()
            norm1_stats(0)
            norm1_scale(0)
            split_low(0)
            norm_low("start", 0, 0)
            split_dt_low()
            selectors()
            zeros()
            conv(0, 0, 0)
            conv(0, 0, 1)
            soft_in("start", 0, 0)
            soft_mid(0)
            conv(0, 0, 2)
            soft_out(0)
            dt_values(0, 0)
            conv(0, 0, 3)
            conv(0, 0, 4)
            s_values("start", 0, 0, 0)
            split_low(1)
            fold_ffn()
            forward_scan("start", 0, 0, None)

            with dve.Fori(0, NB - 1) as it:
                reversed_scan("loop", it, it, it + 1)
                forward_scan("loop", it, it + 1, it)

            b = NB - 1
            reversed_scan("last", 0, b, None)
            bank, used = pj_use(NB, 0, 0)
            dve.wait_ge(pj_full[bank], used + 1)
            dve.tensor_copy(ss[:, 1, :], pj[bank][:, 0:NC]).then_inc(pj_free[bank], 1)
            mix("last", 0, b, 1, 0)
            mix("last", 0, b, 1, 1)
            norm2_stats("last", 0, b)
            norm2_scale(b)
            for c in range(NC):
                feed("last", 0, b, c)

        @block.gpsimd
        def _(pool):
            def keep_x(b):
                pool.wait_ge(x_loaded, 16 * (b + 1))
                pool.tensor_tensor(xres[:], xin[:], bo_sb[:].unsqueeze(1).broadcast_to([P, NC, D]), ALU.add).then_inc(xres_ready, 1)

            def inv_sqrt(src, mid, dst, scale, mid_ready, ready, b):
                alone(pool)
                pool.tensor_scalar(mid, src, scale, EPS, ALU.mult, ALU.add).then_inc(mid_ready, 1)
                pool.wait_ge(mid_ready, b + 1)
                n = mid.shape[-1]
                pool.tensor_tensor(dst, mid, halves[:, 0:n], ALU.pow).then_inc(ready, 1)

            def norm1(b):
                pool.wait_ge(ln1_mv, NC * (b + 1))
                inv_sqrt(mv1[:, :, 1], ve1[:], rstd1[:], 1.0, ln1_ve, ln1_rstd, b)

            def norm2(b):
                pool.wait_ge(ln2_mv, NC * (b + 1))
                inv_sqrt(mv2[:, :, 1], ve2[:], rstd2[:], 1.0, ln2_ve, ln2_rstd, b)

            def root_mean_square(phase, it, b, d):
                bank, used = misc_use(phase, it, f"{d}ss")
                pool.wait_ge(mi_free[bank], used + 2)
                inv_sqrt(ss[:, d, :], ms[:, d, :], rms[:, d, :], 1.0 / DI, ms_ready, rms_ready, 2 * b + d)

            def pieces(b, d):
                u = 2 * b + d
                steps = 2 * PIECES - 2
                pool.wait_ge(s_ready, u + 1)
                left = s_all[:, d, 0]
                n = 0
                for q, rest in enumerate((rem1, rem2, None)):
                    piece = spc[:, :, NH * q:NH * q + NH]
                    alone(pool)
                    pool.tensor_copy(piece, left).then_inc(spc_step if rest is not None else spc_ready, 1)
                    if rest is not None:
                        pool.wait_ge(spc_step, steps * u + n + 1)
                        pool.tensor_tensor(rest[:], left, piece, ALU.subtract).then_inc(spc_step, 1)
                        n += 2
                        pool.wait_ge(spc_step, steps * u + n)
                        left = rest[:]

            def decayed_x(phase, it, b, d, j):
                if j == 0:
                    pool.wait_ge(w_ready, 2 * b + d + 1)
                bank, used = misc_use(phase, it, f"{d}x{j}")
                pool.wait_ge(mi_free[bank], used + 2)
                c = ORDER[d][j]
                o = c * NH
                hq = "p (h q) -> p h q"
                pool.tensor_tensor(xw[:, j, :].rearrange(hq, h=NH), xdt[:, c, :].rearrange(hq, h=NH),
                                   w_end[:, d, o:o + NH].unsqueeze(2).broadcast_to([P, NH, HP]), ALU.mult).then_inc(xw_ready, 1)

            def decayed_c(b, d, p):
                bank, used = sb_use(b, d, f"p{p}")
                pool.wait_ge(sb_free[bank], used + 2)
                if p >= 2:
                    bank, used = py_use(b, d, p - 2)
                    pool.wait_ge(py_full[bank], used + 1)
                pool.tensor_tensor(c2[:, p % 2, LATER[d]], cc[:, d, LATER[d]], es[:, p % 2, LATER[d]], ALU.mult).then_inc(c2_ready, 1)

            def decayed_state(phase, it, b, d, j):
                bank, used = misc_use(phase, it, f"{d}s{j - 1}")
                pool.wait_ge(mi_free[bank], used + 2)
                o = ORDER[d][j] * NH
                pool.tensor_tensor(hs[:].rearrange("p r (e q) -> p (r e) q", e=2),
                                   hst[:, j - 1].rearrange("p r (e q) -> p (r e) q", e=2),
                                   e_end[:, d, o:o + NH].unsqueeze(2).broadcast_to([P, NH, HP]), ALU.mult).then_inc(hs_ready, 1)

            def gate(b, d, p):
                bank, used = py_use(b, d, p)
                pool.wait_ge(py_free[bank], used + 2)
                pool.tensor_tensor(yg[:, d, p, :], yg[:, d, p, :], sz[:, d, p, :], ALU.mult).then_inc(yg_ready, 1)

            def squares(b, d, tiles):
                u = 2 * b + d
                n = 2 * KI - 2
                for t in tiles:
                    pool.wait_ge(yg_ready, KI * u + t + 1)
                    if t >= 2:
                        pool.wait_ge(sq_step, n * u + 2 * t - 1)
                    to = sqsum if t == 0 else sq
                    pool.tensor_tensor(to[:], yg[:, d, t, :], yg[:, d, t, :], ALU.mult).then_inc(sq_step, 1)
                    if t:
                        pool.wait_ge(sq_step, n * u + 2 * t)
                        i = pool.tensor_tensor(sqsum[:], sqsum[:], sq[:], ALU.add)
                        i.then_inc(sqsum_ready if t == KI - 1 else sq_step, 1)

            def result_bias(phase, it, b):
                bank, used = misc_use(phase, it, "1o1")
                pool.wait_ge(mi_free[bank], used + 2)
                pool.wait_ge(out_stored, 16 * NC * b + 1)
                pool.tensor_tensor(ot[:], xres[:], ffb_sb[:].unsqueeze(1).broadcast_to([P, NC, D]), ALU.add).then_inc(otb_ready, 1)

            def scan_start(phase, it, b, d):
                for j in range(NC - 1):
                    decayed_x(phase, it, b, d, j)
                decayed_state(phase, it, b, d, 1)
                decayed_c(b, d, 0)
                decayed_state(phase, it, b, d, 2)

            def reversed_scan(phase, it, b, nxt):
                more = phase == "loop"
                if more:
                    norm1(nxt)
                squares(b, 0, [3])
                scan_start(phase, it, b, 1)
                root_mean_square(phase, it, b, 0)
                decayed_c(b, 1, 1)
                if not more:
                    decayed_c(b, 1, 2)
                    decayed_c(b, 1, 3)
                    return
                gate(b, 1, 0)
                decayed_c(b, 1, 2)
                squares(b, 1, [0])
                gate(b, 1, 1)
                decayed_c(b, 1, 3)
                squares(b, 1, [1])
                gate(b, 1, 2)
                pieces(nxt, 0)
                squares(b, 1, [2])
                gate(b, 1, 3)
                squares(b, 1, [3])

            def forward_scan(phase, it, b, last):
                more = phase == "loop"
                scan_start(phase, it, b, 0)
                if more:
                    root_mean_square(phase, it, last, 1)
                decayed_c(b, 0, 1)
                pieces(b, 1)
                gate(b, 0, 0)
                decayed_c(b, 0, 2)
                if more:
                    norm2(last)
                    result_bias(phase, it, last)
                gate(b, 0, 1)
                decayed_c(b, 0, 3)
                if more:
                    pool.wait_ge(xn2_ready, NC * (last + 1))
                    pool.wait_ge(otb_ready, last + 1)
                    keep_x(b)
                squares(b, 0, [0, 1])
                gate(b, 0, 2)
                squares(b, 0, [2])
                gate(b, 0, 3)

            pool.wait_ge(setup_done, 1)
            norm1(0)
            pool.wait_ge(setup_done, 2)
            pieces(0, 0)
            pool.wait_ge(f_loaded, 16 * 14)
            keep_x(0)
            forward_scan("start", 0, 0, None)

            with pool.Fori(0, NB - 1) as it:
                reversed_scan("loop", it, it, it + 1)
                forward_scan("loop", it, it + 1, it)

            b = NB - 1
            reversed_scan("last", 0, b, None)
            bank, used = pj_use(NB, 0, 0)
            pool.wait_ge(pj_free[bank], used + 2)
            inv_sqrt(ss[:, 1, :], ms[:, 1, :], rms[:, 1, :], 1.0 / DI, ms_ready, rms_ready, 2 * b + 1)
            norm2(b)
            result_bias("last", 0, b)


_DIRS = ("f", "b")
_OUT = ((NB, T, D), "float32")


def _arrays(inputs):
    import numpy as np

    def get(name):
        return np.ascontiguousarray(inputs["L0_" + name])

    tok = np.arange(P)
    consts = np.zeros((P, 4, P), np.float32)
    consts[:, 0] = np.eye(P)
    consts[:, 1] = tok[:, None] <= tok[None, :]
    consts[:, 2] = tok[:, None] >= tok[None, :]
    consts[:, 3] = 1.0
    selcol = np.zeros((P, NH), np.float32)
    for q in range(PIECES):
        for h in range(NH):
            selcol[NH * q + h, h] = 1.0

    tiles = [KI] + list(range(KI))
    arrays = {"x": get("attn_x"), "consts": consts, "selcol": selcol}
    for s in _DIRS:
        arrays[s + "win"] = get(f"attn_{s}Win")
        arrays[s + "convw"] = get(f"attn_{s}convw").reshape(KW, NCONV, P).transpose(2, 1, 0)[:, tiles]
        arrays[s + "convb"] = get(f"attn_{s}convb").reshape(NCONV, P).transpose(1, 0)[:, tiles]
        arrays[s + "dtb"] = get(f"attn_{s}dtb")
        arrays[s + "alog"] = get(f"attn_{s}Alog")
        arrays[s + "dskip"] = get(f"attn_{s}D").reshape(KI, 2).transpose(1, 0)
        arrays[s + "normw"] = get(f"attn_{s}normw").reshape(KI, P).transpose(1, 0)
        arrays[s + "woutT"] = get(f"attn_{s}Wout").transpose(1, 0)
    arrays |= {"wo": get("attn_Wo"), "bo": get("attn_bo"), "ffT": get("ffn_W").transpose(1, 0), "ffb": get("ffn_b"),
               "vrT": get("ffn_V_r").transpose(1, 0), "cT": get("ffn_C").transpose(1, 0)}
    return {k: np.ascontiguousarray(v) for k, v in arrays.items()}


def kernel(**inputs):
    import numpy as np
    import concourse.bacc as bacc
    from concourse.bass_utils import run_bass_kernel_spmd

    nc = bacc.Bacc("TRN2", target_bir_lowering=False, num_devices=1)
    arrays = {f"in_{k}": v for k, v in _arrays(inputs).items()}
    ap = {k[3:]: nc.dram_tensor(k, v.shape, mybir.dt.from_np(v.dtype), kind="ExternalInput").ap() for k, v in arrays.items()}
    out = nc.dram_tensor("out", _OUT[0], mybir.dt.from_np(np.dtype(_OUT[1])), kind="ExternalOutput").ap()

    def both(name):
        return [ap[s + name] for s in _DIRS]

    build(nc, ap["x"], ap["consts"], ap["selcol"], both("win"), both("convw"), both("convb"), both("dtb"), both("alog"),
          both("dskip"), both("normw"), both("woutT"), ap["wo"], ap["bo"], ap["ffT"], ap["ffb"], ap["vrT"], ap["cT"], out)
    result = run_bass_kernel_spmd(nc, [arrays], core_ids=[0])
    return result.results[0]["out"]
```
